# Optimizing a Trainium2 kernel written in Bass

```python
import numpy as np
import jax
import jax.numpy as jnp

def _softmax(x, axis=-1):
    return jax.nn.softmax(x, axis=axis)

def _gelu(x):
    return jax.nn.gelu(x, approximate=True)

def _silu(x):
    return jax.nn.silu(x)

def _sigmoid(x):
    return jax.nn.sigmoid(x)

def _layernorm(x, axis=-1, eps=1e-05):
    m = jnp.mean(x, axis=axis, keepdims=True)
    v = jnp.var(x, axis=axis, keepdims=True)
    return (x - m) / jnp.sqrt(v + eps)

def _scatter_add(tgt, idx, src, axis=0):
    return tgt.at[idx].add(src)

def _segment_sum(src, seg, n):
    return jax.ops.segment_sum(src, seg, n)
kernel_name = 'mk_cond_resid_d2_seqx_r4_c8823d'

def setup_inputs(seed: int=0):
    np.random.seed(seed)
    _w = jnp.asarray

    def _rec_inputs():
        import jax
        import jax.numpy as jnp
        _rk = jax.random.key(seed)
        x = -0.000125 + 0.9999 * jax.random.normal(jax.random.fold_in(_rk, 1), (8, 256, 1024), jnp.float32)
        _lenS = 256 - jax.random.randint(jax.random.fold_in(_rk, 7), (8,), 0, max(1, 256 // 4) + 1, jnp.int32)
        _lenS2 = 256 - jax.random.randint(jax.random.fold_in(_rk, 8), (8,), 0, max(1, 256 // 4) + 1, jnp.int32)
        condB_codebook = -0.0625 + 0.715345 * jax.random.normal(jax.random.fold_in(_rk, 11), (8,), jnp.float32)
        itok_B_0_15 = jax.random.randint(jax.random.fold_in(_rk, 12), (8,), 0, 16, jnp.int32)
        return (x, condB_codebook, itok_B_0_15)
    x, condB_codebook, itok_B_0_15 = _rec_inputs()

    def _L0_cond_setup():
        import jax, jax.numpy as jnp
        import numpy as np
        GROUP = 128
        LORA_ALPHA = 32.0
        LORA_RANK = 64
        key = jax.random.key(seed)
        k1, k2, k3, k4 = jax.random.split(key, 4)
        O, I = (1024, 1024)
        x = jax.random.normal(k1, (4, 512, I), dtype=jnp.float32)
        weight = jax.random.normal(k2, (O, I), dtype=jnp.float32) * 0.02
        wg = weight.reshape(O, I // GROUP, GROUP)
        scale_log = jnp.log(jnp.clip(jnp.max(jnp.abs(wg), axis=2, keepdims=True), 1e-05))
        codebook = jnp.array([-1.0, -0.25, 0.0, 1.0], dtype=jnp.float32)
        lora_A = jax.random.normal(k3, (LORA_RANK, I), dtype=jnp.float32) * 0.02
        lora_B = jax.random.normal(k4, (O, LORA_RANK), dtype=jnp.float32) * 0.02
        return {'x': x, 'weight': weight, 'scale_log': scale_log, 'codebook': codebook, 'lora_A': lora_A, 'lora_B': lora_B}
    _L0_cond_all = _L0_cond_setup()
    _L0_cond_in = {k: v for k, v in _L0_cond_all.items() if k in ('weight', 'scale_log', 'lora_A', 'lora_B')}
    del _L0_cond_all

    def _L1_cond_setup():
        import jax, jax.numpy as jnp
        import numpy as np
        SCALING = 16.0 / 16
        key = jax.random.key(seed)
        k1, k2, k3, k4, k5 = jax.random.split(key, 5)
        B, S, D_IN, D_OUT, R, N_ADPT = (8, 512, 1024, 1024, 16, 16)
        x = jax.random.normal(k1, (B, S, D_IN), dtype=jnp.float32)
        adapter_indices = jax.random.randint(k2, (B,), 0, N_ADPT, dtype=jnp.int32)
        W = jax.random.normal(k3, (D_IN, D_OUT), dtype=jnp.float32) * 0.02
        lora_A = jax.random.normal(k4, (N_ADPT, D_IN, R), dtype=jnp.float32) * 0.02
        lora_B = jax.random.normal(k5, (N_ADPT, R, D_OUT), dtype=jnp.float32) * 0.02
        return {'x': x, 'adapter_indices': adapter_indices, 'W': W, 'lora_A': lora_A, 'lora_B': lora_B}
    _L1_cond_all = _L1_cond_setup()
    _L1_cond_in = {k: v for k, v in _L1_cond_all.items() if k in ('W', 'lora_A', 'lora_B')}
    del _L1_cond_all
    return {'x': x, 'condB_codebook': condB_codebook, 'itok_B_0_15': itok_B_0_15, 'L0_cond_weight': _L0_cond_in['weight'], 'L0_cond_scale_log': _L0_cond_in['scale_log'], 'L0_cond_lora_A': _L0_cond_in['lora_A'], 'L0_cond_lora_B': _L0_cond_in['lora_B'], 'L1_cond_W': _L1_cond_in['W'], 'L1_cond_lora_A': _L1_cond_in['lora_A'], 'L1_cond_lora_B': _L1_cond_in['lora_B']}

def reference(x, condB_codebook, itok_B_0_15, L0_cond_weight, L0_cond_scale_log, L0_cond_lora_A, L0_cond_lora_B, L1_cond_W, L1_cond_lora_A, L1_cond_lora_B):
    import jax
    import jax.numpy as jnp

    def _L0_cond_ref(x, weight, scale_log, codebook, lora_A, lora_B):
        import jax, jax.numpy as jnp
        import numpy as np
        GROUP = 128
        LORA_ALPHA = 32.0
        LORA_RANK = 64
        O, I = weight.shape
        lora_delta = lora_B @ lora_A * (LORA_ALPHA / LORA_RANK)
        cb = codebook / jnp.clip(jnp.max(jnp.abs(codebook)), 1e-08)
        scale = jnp.exp(scale_log)
        wg = (weight + lora_delta).reshape(O, I // GROUP, GROUP)
        normalized = wg / scale
        thresholds = (cb[:-1] + cb[1:]) * 0.5
        idx = jnp.searchsorted(thresholds, normalized, side='left')
        quantized = cb[idx]
        w = jax.lax.stop_gradient(quantized - normalized) + normalized
        w_q = (w * scale).reshape(O, I)
        w_eff = w_q + lora_delta
        return x @ w_eff.T

    def _L1_cond_ref(x, adapter_indices, W, lora_A, lora_B):
        import jax, jax.numpy as jnp
        import numpy as np
        SCALING = 16.0 / 16
        base_out = jnp.einsum('bsi,io->bso', x, W)
        A = lora_A[adapter_indices]
        Bm = lora_B[adapter_indices]
        xr = jnp.einsum('bsi,bir->bsr', x, A)
        lora_out = jnp.einsum('bsr,bro->bso', xr, Bm)
        return base_out + lora_out * SCALING
    x = x + _L0_cond_ref(x, L0_cond_weight, L0_cond_scale_log, condB_codebook, L0_cond_lora_A, L0_cond_lora_B)
    x = x + _L1_cond_ref(x, itok_B_0_15, L1_cond_W, L1_cond_lora_A, L1_cond_lora_B)
    return x

_drawn_inputs = setup_inputs


def setup_inputs(seed=0):
    import zlib

    import numpy as np

    out = dict(_drawn_inputs(seed))
    spreads = {}
    factors = {}
    for name, (base, spread) in spreads.items():
        noise = np.random.default_rng([zlib.crc32(name.encode()), seed]).standard_normal(out[name].shape)
        drawn = base * np.exp(spread * noise) if base else spread * noise
        out[name] = jnp.asarray(drawn.astype(out[name].dtype))
    for name, factor in factors.items():
        out[name] = (out[name] * factor).astype(out[name].dtype)
    return out
```

```python
import concourse.bass as bass
from concourse import mybir
from contextlib import ExitStack

P = 128


def two_layers(nc, xT, codebook, adapter, weightT, scale_log, lora0_a, lora0_bT, w1, lora1_a, lora1_b, out):
    f32, f32r, i32, u8 = mybir.dt.float32, mybir.dt.float32r, mybir.dt.int32, mybir.dt.uint8
    ALU, ACT, AX = mybir.AluOpType, mybir.ActivationFunctionType, mybir.AxisListType

    NB = xT.shape[0]
    D = w1.shape[0]
    DT = D // P
    TOK = xT.shape[2] // DT
    TT = TOK // P
    NA, _, _, R1 = lora1_a.shape
    R0 = lora0_bT.shape[0]
    G = scale_log.shape[1] // DT
    HB = D // 2
    QI = 2
    QC = QI * P
    OP = 2
    NQ = DT // QI
    NJ = DT // OP
    STEPS = NQ * NJ
    SE = OP * QC
    NL = codebook.shape[1]
    assert 2 * R0 == P and NB * R1 == P and 8 * R1 == P and OP * QC == 512 and NL == 8 and G == DT

    ctx = ExitStack()

    def sem(name):
        return ctx.enter_context(nc.semaphore(name))

    def sb(stack, name, shape, dt):
        return stack.enter_context(nc.sbuf_tensor(name, shape, dt))

    with ctx:
        m_hi = sb(ctx, "m_hi", [P, DT, D], f32r)
        m_lo = sb(ctx, "m_lo", [P, DT, D], f32r)
        u_hi = sb(ctx, "u_hi", [P, DT, NB * R1], f32r)
        u_lo = sb(ctx, "u_lo", [P, DT, NB * R1], f32r)

        one = ExitStack()
        a0_hi = sb(one, "a0_hi", [P, D], f32r)
        a0_lo = sb(one, "a0_lo", [P, D], f32r)
        b0_hl = sb(one, "b0_hl", [P, D], f32r)
        delta = sb(one, "delta", [P, 3, SE], f32)
        wraw = sb(one, "wraw", [P, 2, OP, QC], f32)
        norm = sb(one, "norm", [P, 3, SE], f32)
        quan = sb(one, "quan", [P, 3, SE], f32)
        upper = sb(one, "upper", [P, SE], f32)
        mask = sb(one, "mask", [P, 2, NL - 1, SE], u8)
        stage = sb(one, "stage", [P, 2, D], f32)
        a1_hi = sb(one, "a1_hi", [P, DT, NB * R1], f32r)
        a1_lo = sb(one, "a1_lo", [P, DT, NB * R1], f32r)
        ident = sb(one, "ident", [P, P], f32)
        ident_r = sb(one, "ident_r", [P, P], f32r)
        cbn = sb(one, "cbn", [P, NL], f32)
        cbt = sb(one, "cbt", [P, NL], f32)
        cbmax = sb(one, "cbmax", [P, 2], f32)
        thr = sb(one, "thr", [P, NL - 1], f32)
        brk = sb(one, "brk", [P, NL - 1], f32)
        negbrk = sb(one, "negbrk", [P, NL - 1], f32)
        scale = sb(one, "scale", [P, DT * G], f32)
        rscale = sb(one, "rscale", [P, DT * G], f32)
        ex = sb(one, "ex", [P, 3, DT * G], f32)
        ki = sb(one, "ki", [P, 2, DT * G], i32)
        kb = sb(one, "kb", [P, 2, DT * G], i32)
        weff_hi = sb(one, "weff_hi", [P, 2, OP, QC], f32r)
        weff_lo = sb(one, "weff_lo", [P, 2, OP, QC], f32r)
        ut = sb(one, "ut", [P, QC], f32)
        w_hi = sb(one, "w_hi", [P, DT, D], f32r)
        w_lo = sb(one, "w_lo", [P, DT, D], f32r)
        one.close()

        x_raw = sb(ctx, "x_raw", [P, 2, DT * TOK], f32)
        b_raw = sb(ctx, "b_raw", [P, D], f32)
        x_hi = sb(ctx, "x_hi", [P, 2, DT, TOK], f32r)
        x_lo = sb(ctx, "x_lo", [P, 2, DT, TOK], f32r)
        b_hl = sb(ctx, "b_hl", [P, 2, D], f32r)
        u_st = sb(ctx, "u_st", [P, 2, DT, 4, 2, R1], f32r)
        p_hl = sb(ctx, "p_hl", [P, 2, TOK], f32r)
        y = sb(ctx, "y", [P, 2, D], f32)

        acc = [ctx.enter_context(nc.psum_tensor(f"acc{i}", [P, HB], f32)) for i in range(4)]
        ps_u = ctx.enter_context(nc.psum_tensor("ps_u", [P, HB], f32))
        ps_t = ctx.enter_context(nc.psum_tensor("ps_t", [P, HB], f32))
        ps_d = [ctx.enter_context(nc.psum_tensor(f"ps_d{i}", [P, OP, QC], f32)) for i in range(2)]

        codebook_in = sem("codebook_in")
        scale_log_in = sem("scale_log_in")
        staged_in = [sem(f"staged_in{i}") for i in range(2)]
        weight_in = [sem(f"weight_in{i}") for i in range(2)]
        x_in = [sem(f"x_in{i}") for i in range(2)]
        b_in = sem("b_in")
        y_out = [sem(f"y_out{i}") for i in range(2)]
        ident_made = sem("ident_made")
        brk_ready = sem("brk_ready")
        scale_ready = sem("scale_ready")
        diag_added = sem("diag_added")
        hi_made = sem("hi_made")
        lo_made_v = sem("lo_made_v")
        lo_made_g = sem("lo_made_g")
        vchain = sem("vchain")
        gchain = sem("gchain")
        delta_mm = sem("delta_mm")
        delta_sb = sem("delta_sb")
        wsum = sem("wsum")
        norm_ready = sem("norm_ready")
        mask_ready = sem("mask_ready")
        select_done = sem("select_done")
        weff_ready = sem("weff_ready")
        weff_hi_ready = sem("weff_hi_ready")
        weff_lo_ready = sem("weff_lo_ready")
        weff_used = sem("weff_used")
        m_acc = sem("m_acc")
        m_hi_ready = sem("m_hi_ready")
        m_lo_ready = sem("m_lo_ready")
        ut_mm = sem("ut_mm")
        ut_sb = sem("ut_sb")
        u_back = sem("u_back")
        u_hi_ready = sem("u_hi_ready")
        u_lo_ready = sem("u_lo_ready")
        x_hi_ready = sem("x_hi_ready")
        x_lo_ready = sem("x_lo_ready")
        b_hi_ready = sem("b_hi_ready")
        b_lo_ready = sem("b_lo_ready")
        u_st_ready = sem("u_st_ready")
        p_mm = sem("p_mm")
        p_hi_ready = sem("p_hi_ready")
        p_lo_ready = sem("p_lo_ready")
        y_mm = sem("y_mm")
        y_act = sem("y_act")
        y_dve = sem("y_dve")

        block = ctx.enter_context(nc.Block())

        STAGED = ["b0", "a0"] + [("w", t) for t in range(4)] + ["a1"] + [("w", t) for t in range(4, DT)]
        POOL_W = 4
        AT = {item: n for n, item in enumerate(STAGED)}
        LOADS_OF = [2, 2] + [1] * 4 + [NB] + [1] * (DT - 4)

        MASK_ORDER = [0, 4, 1, 5, 2, 6, 3]

        def by_pool(item):
            return item[0] == "w" and item[1] < POOL_W

        def stage_wait(eng, item):
            n = AT[item]
            eng.wait_ge(staged_in[n % 2], 16 * sum(LOADS_OF[n % 2:n + 1:2]))

        def low_count(item):
            same = [i for i in STAGED if by_pool(i) == by_pool(item)]
            return same.index(item) + 1

        def low_wait(eng, item):
            eng.wait_ge(lo_made_g if by_pool(item) else lo_made_v, low_count(item))

        def quarter_view(t3):
            return t3.rearrange("p (g c) -> p g c", c=P)

        @block.sync
        def _(sp):
            sp.dma_start(cbt[:], codebook).then_inc(codebook_in, 16)
            for n, item in enumerate(STAGED):
                if n >= 2:
                    sp.wait_ge(hi_made, n - 1)
                    low_wait(sp, STAGED[n - 2])
                s, done = stage[:, n % 2, :], staged_in[n % 2]
                if item == "b0":
                    sp.dma_start(s[0:R0, :], lora0_bT).then_inc(done, 16)
                    sp.dma_start(s[R0:P, :], lora0_bT).then_inc(done, 16)
                elif item == "a0":
                    sp.dma_start(s[0:R0, :], lora0_a).then_inc(done, 16)
                    sp.dma_start(s[R0:P, :], lora0_a).then_inc(done, 16)
                    sp.dma_start(ex[:, 0, :], scale_log).then_inc(scale_log_in, 16)
                elif item == "a1":
                    s4 = s.rearrange("p (t b r) -> p t b r", t=DT, b=NB)
                    for b in range(NB):
                        e = sp.value_load(adapter[0:1, b:b + 1], min_val=0, max_val=NA - 1)
                        sp.dma_start(s4[:, :, b, :], lora1_a[bass.ds(e, 1), :, :, :].rearrange(
                            "a p t r -> (a p) t r")).then_inc(done, 16)
                else:
                    t = item[1]
                    sp.dma_start(s, w1[t * P:(t + 1) * P, :]).then_inc(done, 16)

            def load_x(b, slot):
                sp.dma_start(x_raw[:, slot, :], xT[bass.ds(b, 1), :, :].rearrange(
                    "b p c -> (b p) c")).then_inc(x_in[slot], 16)

            def load_b(b):
                e = sp.value_load(adapter[0:1, bass.ds(b, 1)], min_val=0, max_val=NA - 1)
                src = lora1_b[bass.ds(e, 1), :, :].rearrange("a r n -> (a r) n")
                for g in range(P // R1):
                    sp.dma_start(b_raw[g * R1:(g + 1) * R1, :], src).then_inc(b_in, 16)

            def store(b, tt, done):
                sp.wait_ge(y_act, done)
                sp.wait_ge(y_dve, done)
                sp.dma_start(out[bass.ds(b * TT + tt, 1), :, :].rearrange("t p n -> (t p) n"),
                             y[:, tt, :]).then_inc(y_out[tt], 16)

            sp.wait_ge(delta_mm, STEPS)
            sp.wait_ge(weff_ready, STEPS)
            load_x(0, 0)
            sp.wait_ge(weff_lo_ready, STEPS)
            sp.wait_ge(weff_hi_ready, STEPS)
            load_x(1, 1)
            load_b(0)
            for b in range(NB):
                if b + 1 < NB:
                    sp.wait_ge(b_hi_ready, b + 1)
                    sp.wait_ge(b_lo_ready, b + 1)
                    load_b(b + 1)
                if b + 2 < NB:
                    sp.wait_ge(x_hi_ready, b + 1)
                    sp.wait_ge(x_lo_ready, b + 1)
                    load_x(b + 2, b % 2)
                for tt in range(TT):
                    store(b, tt, b * TT + tt + 1)
            for tt in range(TT):
                sp.wait_ge(y_out[tt], 16 * NB)

        @block.gpsimd
        def _(pool):
            g = nc.gpsimd
            chain = [0]

            def link(ins):
                chain[0] += 1
                ins.then_inc(gchain, 1)
                pool.wait_ge(gchain, chain[0])

            link(g.memset(ident[:], 0.0))
            g.affine_select(out=ident[:], in_=ident[:], compare_op=ALU.not_equal, fill=1.0, base=0,
                            pattern=[[-1, P]], channel_multiplier=1).then_inc(ident_made, 1)
            pool.wait_ge(ident_made, 1)

            def load_weight(k):
                q, j = k // NJ, k % NJ
                if k >= 2:
                    pool.wait_ge(wsum, k - 1)
                g.dma_start(wraw[:, k % 2, :, :], weightT[j, :, :, q * QC:(q + 1) * QC]
                            ).then_inc(weight_in[k % 2], 16)

            load_weight(0)
            load_weight(1)

            def diag(t):
                stage_wait(pool, ("w", t))
                d = stage[:, AT[("w", t)] % 2, t * P:(t + 1) * P]
                g.tensor_tensor(d, d, ident[:], ALU.add).then_inc(diag_added, 1)

            def low(t):
                n = AT[("w", t)]
                pool.wait_ge(diag_added, t + 1)
                pool.wait_ge(hi_made, n + 1)
                g.tensor_tensor(w_lo[:, t, :], stage[:, n % 2, :], w_hi[:, t, :].bitcast(f32),
                                ALU.subtract).then_inc(lo_made_g, 1)

            for t in range(0, POOL_W, 2):
                diag(t)
                diag(t + 1) if t == 0 else None
                low(t)
                diag(t + 1) if t else None
                low(t + 1)

            def sc(k):
                q, j = k // NJ, k % NJ
                s = scale[:].rearrange("p (t g) -> p t g", g=G)[:, j * OP:(j + 1) * OP, q * QI:(q + 1) * QI]
                return s.unsqueeze(3).broadcast_to([P, OP, QI, P])

            def dequantise(k):
                v = quan[:, k % 3, :]
                v4 = v.rearrange("p (t g c) -> p t g c", t=OP, g=QI)
                pool.wait_ge(select_done, 9 * (k + 1))
                link(g.tensor_tensor(v, v, norm[:, k % 3, :], ALU.subtract))
                link(g.tensor_tensor(v, v, norm[:, k % 3, :], ALU.add))
                link(g.tensor_tensor(v4, v4, sc(k), ALU.mult))
                pool.wait_ge(delta_sb, k + 1)
                g.tensor_tensor(v, v, delta[:, k % 3, :], ALU.add).then_inc(weff_ready, 1)

            def low_weff(k):
                pool.wait_ge(weff_hi_ready, k + 1)
                if k >= 2:
                    pool.wait_ge(weff_used, k - 1)
                g.tensor_tensor(weff_lo[:, k % 2, :, :].rearrange("p t c -> p (t c)"), quan[:, k % 3, :],
                                weff_hi[:, k % 2, :, :].rearrange("p t c -> p (t c)").bitcast(f32),
                                ALU.subtract).then_inc(weff_lo_ready, 1)

            pool.wait_ge(scale_ready, 1)
            for k in range(STEPS):
                if k:
                    low_weff(k - 1)
                if k + 2 < STEPS:
                    load_weight(k + 2)
                dequantise(k)
            low_weff(STEPS - 1)

        @block.scalar
        def _(act):
            a = nc.scalar

            def high(item, dst):
                n = AT[item]
                stage_wait(act, item)
                if item[0] == "w":
                    act.wait_ge(diag_added, item[1] + 1)
                a.activation(dst, stage[:, n % 2, :], ACT.Copy).then_inc(hi_made, 1)

            def copy_delta(k):
                act.wait_ge(delta_mm, k + 1)
                if k >= 3:
                    act.wait_ge(weff_ready, k - 2)
                a.activation(delta[:, k % 3, :], ps_d[k % 2][:].rearrange("p t c -> p (t c)"), ACT.Copy,
                             scale=0.5).then_inc(delta_sb, 1)

            def masks(k):
                act.wait_ge(norm_ready, k + 1)
                if k >= 2:
                    act.wait_ge(select_done, 9 * (k - 1))
                for i in MASK_ORDER:
                    a.activation(mask[:, k % 2, i, :], norm[:, k % 3, :], ACT.Sign,
                                 bias=negbrk[:, i:i + 1]).then_inc(mask_ready, 1)

            def high_weff(k):
                act.wait_ge(weff_ready, k + 1)
                if k >= 2:
                    act.wait_ge(weff_used, k - 1)
                    act.wait_ge(weff_lo_ready, k - 1)
                a.activation(weff_hi[:, k % 2, :, :].rearrange("p t c -> p (t c)"), quan[:, k % 3, :],
                             ACT.Copy).then_inc(weff_hi_ready, 1)

            def high_m(q):
                for i in range(QI):
                    for h in range(2):
                        act.wait_ge(m_acc, 4 * q + 2 * i + h + 1)
                        a.activation(m_hi[:, q * QI + i, h * HB:(h + 1) * HB], acc[2 * i + h][:],
                                     ACT.Copy).then_inc(m_hi_ready, 1)

            def take_ut(q):
                act.wait_ge(ut_mm, q + 1)
                if q:
                    act.wait_ge(u_back, q)
                a.activation(ut[:], ps_u[:, 0:QC], ACT.Copy).then_inc(ut_sb, 1)

            def high_u(q):
                act.wait_ge(u_back, q + 1)
                a.activation(u_hi[:, q * QI:(q + 1) * QI, :],
                             ps_t[:, 0:QC].rearrange("p (t c) -> p t c", t=QI), ACT.Copy).then_inc(u_hi_ready, 1)

            high("b0", b0_hl[:])
            high("a0", a0_hi[:])
            act.wait_ge(ident_made, 1)
            a.activation(ident_r[:], ident[:], ACT.Copy).then_inc(ident_made, 1)
            high(("w", 0), w_hi[:, 0, :])
            high(("w", 1), w_hi[:, 1, :])
            high(("w", 2), w_hi[:, 2, :])
            high(("w", 3), w_hi[:, 3, :])
            copy_delta(0)
            act.wait_ge(brk_ready, 1)
            for k in range(STEPS + 2):
                if k + 1 < STEPS:
                    copy_delta(k + 1)
                if k < STEPS:
                    masks(k)
                if k == 0:
                    high("a1", a1_hi[:].rearrange("p t c -> p (t c)"))
                    high(("w", 4), w_hi[:, 4, :])
                if k == 1:
                    high(("w", 5), w_hi[:, 5, :])
                    high(("w", 6), w_hi[:, 6, :])
                if k == 2:
                    high(("w", 7), w_hi[:, 7, :])
                if k >= 2:
                    high_weff(k - 2)
                if k >= 2 + NJ and (k - 2) % NJ == 0:
                    high_m((k - 2) // NJ - 1)
                    take_ut((k - 2) // NJ - 1)
                if k >= 3 + NJ and (k - 3) % NJ == 0:
                    high_u((k - 3) // NJ - 1)

            def high_x(b):
                act.wait_ge(x_in[b % 2], 16 * (b // 2 + 1))
                if b >= 2:
                    act.wait_ge(y_mm, 2 * TT * (b - 1))
                a.activation(x_hi[:, b % 2, :, :].rearrange("p t c -> p (t c)"), x_raw[:, b % 2, :],
                             ACT.Copy).then_inc(x_hi_ready, 1)

            def high_b(b):
                act.wait_ge(b_in, 16 * (P // R1) * (b + 1))
                if b >= 2:
                    act.wait_ge(y_mm, 2 * TT * (b - 1))
                a.activation(b_hl[:, b % 2, :], b_raw[:], ACT.Copy).then_inc(b_hi_ready, 1)

            def stack_u(b):
                if b >= 2:
                    act.wait_ge(p_mm, b - 1)
                for c, u in enumerate((u_hi, u_lo)):
                    src = u[:, :, b * R1:(b + 1) * R1].bitcast(f32).unsqueeze(2).broadcast_to([P, DT, 4, R1])
                    a.activation(u_st[:, b % 2, :, :, c, :], src, ACT.Copy).then_inc(u_st_ready, 1)

            act.wait_ge(weff_lo_ready, STEPS)
            high_x(0)
            high_m(NQ - 1)
            take_ut(NQ - 1)
            high_u(NQ - 1)
            act.wait_ge(u_hi_ready, NQ)
            act.wait_ge(u_lo_ready, NQ)
            stack_u(0)
            high_b(0)
            for b in range(NB):
                if b + 1 < NB:
                    high_x(b + 1)
                    stack_u(b + 1)
                act.wait_ge(p_mm, b + 1)
                if b >= 2:
                    act.wait_ge(y_mm, 2 * TT * (b - 1))
                a.activation(p_hl[:, b % 2, :], ps_u[:, 0:TOK], ACT.Copy).then_inc(p_hi_ready, 1)
                if b + 1 < NB:
                    high_b(b + 1)
                for tt in range(TT):
                    act.wait_ge(y_mm, 2 * (b * TT + tt) + 1)
                    if b:
                        act.wait_ge(y_out[tt], 16 * b)
                    a.activation(y[:, tt, 0:HB], acc[2 * tt][:], ACT.Copy).then_inc(y_act, 1)

        @block.vector
        def _(dve):
            v = nc.vector
            chain = [0]

            def link(ins):
                chain[0] += 1
                ins.then_inc(vchain, 1)
                dve.wait_ge(vchain, chain[0])

            def low(item, dst, rows=slice(0, P), hi=None):
                n = AT[item]
                dve.wait_ge(hi_made, n + 1)
                v.tensor_tensor(dst, stage[rows, n % 2, :], hi, ALU.subtract).then_inc(lo_made_v, 1)

            dve.wait_ge(codebook_in, 16)
            link(v.tensor_scalar(cbn[:], cbt[:], -1.0, None, ALU.mult))
            link(v.tensor_tensor(cbn[:], cbn[:], cbt[:], ALU.max))
            link(v.reduce_max(cbmax[:, 0:1], cbn[:], AX.X))
            link(v.tensor_scalar(cbmax[:, 0:1], cbmax[:, 0:1], 1e-8, None, ALU.max))
            link(v.reciprocal(cbmax[:, 1:2], cbmax[:, 0:1]))
            link(v.tensor_scalar(cbn[:], cbt[:], cbmax[:, 1:2], None, ALU.mult))
            link(v.tensor_tensor(thr[:], cbn[:, 0:NL - 1], cbn[:, 1:NL], ALU.add))
            link(v.tensor_scalar(thr[:], thr[:], 0.5, None, ALU.mult))
            link(v.tensor_copy(brk[:, 3:4], thr[:, 3:4]))
            link(v.tensor_tensor(brk[:, 1:2], thr[:, 1:2], brk[:, 3:4], ALU.min))
            link(v.tensor_tensor(brk[:, 5:6], thr[:, 5:6], brk[:, 3:4], ALU.max))
            link(v.tensor_tensor(brk[:, 2:5:2], thr[:, 2:5:2], brk[:, 1:4:2], ALU.max))
            link(v.tensor_tensor(brk[:, 2:5:2], brk[:, 2:5:2], brk[:, 3:6:2], ALU.min))
            link(v.tensor_tensor(brk[:, 0:1], thr[:, 0:1], brk[:, 1:2], ALU.min))
            link(v.tensor_tensor(brk[:, 6:7], thr[:, 6:7], brk[:, 5:6], ALU.max))
            v.tensor_scalar(negbrk[:], brk[:], -1.0, None, ALU.mult).then_inc(brk_ready, 1)

            low("b0", b0_hl[R0:P, :], slice(R0, P), b0_hl[R0:P, :].bitcast(f32))
            low("a0", a0_lo[:], hi=a0_hi[:].bitcast(f32))

            x_, r_, p_ = ex[:, 0, :], ex[:, 1, :], ex[:, 2, :]
            dve.wait_ge(scale_log_in, 16)
            link(v.tensor_scalar(x_, x_, -104.0, 89.5, ALU.max, ALU.min))
            link(v.tensor_scalar(ki[:, 1, :], x_, 1.4426950408889634, None, ALU.mult))
            link(v.tensor_copy(p_, ki[:, 1, :]))
            link(v.scalar_tensor_tensor(out=r_, in0=p_, scalar=-0.693359375, in1=x_, op0=ALU.mult, op1=ALU.add))
            link(v.scalar_tensor_tensor(out=r_, in0=p_, scalar=2.12194440e-4, in1=r_, op0=ALU.mult, op1=ALU.add))
            link(v.tensor_scalar(p_, r_, 1.0 / 5040, None, ALU.mult))
            for c in (1.0 / 720, 1.0 / 120, 1.0 / 24, 1.0 / 6, 0.5, 1.0):
                link(v.scalar_tensor_tensor(out=p_, in0=p_, scalar=c, in1=r_, op0=ALU.add, op1=ALU.mult))
            link(v.tensor_scalar(p_, p_, 1.0, None, ALU.add))
            link(v.tensor_scalar(ki[:, 0, :], ki[:, 1, :], 1, None, ALU.arith_shift_right))
            link(v.tensor_tensor(ki[:, 1, :], ki[:, 1, :], ki[:, 0, :], ALU.subtract))
            link(v.tensor_scalar(kb[:], ki[:], 127.0, None, ALU.add))
            link(v.tensor_scalar(kb[:], kb[:], 23, None, ALU.logical_shift_left))
            link(v.tensor_tensor(p_, p_, kb[:, 0, :].bitcast(f32), ALU.mult))
            link(v.tensor_tensor(scale[:], p_, kb[:, 1, :].bitcast(f32), ALU.mult))
            v.reciprocal(rscale[:], scale[:]).then_inc(scale_ready, 1)
            dve.wait_ge(scale_ready, 1)

            def normalise(k):
                q, j = k // NJ, k % NJ
                dve.wait_ge(delta_sb, k + 1)
                dve.wait_ge(weight_in[k % 2], 16 * (k // 2 + 1))
                if k >= 3:
                    dve.wait_ge(weff_ready, k - 2)
                n = norm[:, k % 3, :]
                v.tensor_tensor(n, delta[:, k % 3, :], wraw[:, k % 2, :, :].rearrange("p t c -> p (t c)"),
                                ALU.add).then_inc(wsum, 1)
                dve.wait_ge(wsum, k + 1)
                n4 = n.rearrange("p (t g c) -> p t g c", t=OP, g=QI)
                r = rscale[:].rearrange("p (t g) -> p t g", g=G)[:, j * OP:(j + 1) * OP, q * QI:(q + 1) * QI]
                v.tensor_tensor(n4, n4, r.unsqueeze(3).broadcast_to([P, OP, QI, P]),
                                ALU.mult).then_inc(norm_ready, 1)

            def select(k):
                lower = quan[:, k % 3, :]
                if k >= 3:
                    dve.wait_ge(weff_lo_ready, k - 2)
                    dve.wait_ge(weff_hi_ready, k - 2)
                done = 9 * k
                if k:
                    dve.wait_ge(select_done, done)
                v.tensor_copy(lower, cbn[:, 0:1].broadcast_to([P, SE])).then_inc(select_done, 1)
                v.tensor_copy(upper[:], cbn[:, 4:5].broadcast_to([P, SE])).then_inc(select_done, 1)
                done += 2
                for n, i in enumerate(MASK_ORDER):
                    dve.wait_ge(mask_ready, 7 * k + n + 1)
                    dve.wait_ge(select_done, done + n - 1 + (i == 3))
                    dst = upper[:] if i > 3 else lower
                    data = upper[:] if i == 3 else cbn[:, i + 1:i + 2].broadcast_to([P, SE])
                    v.copy_predicated(dst, mask[:, k % 2, i, :], data).then_inc(select_done, 1)

            def low_m(q):
                for i in range(QI):
                    for h in range(2):
                        n = 4 * q + 2 * i + h + 1
                        dve.wait_ge(m_hi_ready, n)
                        s = slice(h * HB, (h + 1) * HB)
                        v.tensor_tensor(m_lo[:, q * QI + i, s], acc[2 * i + h][:],
                                        m_hi[:, q * QI + i, s].bitcast(f32), ALU.subtract).then_inc(m_lo_ready, 1)

            def low_u(q):
                dve.wait_ge(u_hi_ready, q + 1)
                v.tensor_tensor(u_lo[:, q * QI:(q + 1) * QI, :],
                                ps_t[:, 0:QC].rearrange("p (t c) -> p t c", t=QI),
                                u_hi[:, q * QI:(q + 1) * QI, :].bitcast(f32), ALU.subtract).then_inc(u_lo_ready, 1)

            def diag(t):
                stage_wait(dve, ("w", t))
                dve.wait_ge(diag_added, t)
                d = stage[:, AT[("w", t)] % 2, t * P:(t + 1) * P]
                v.tensor_tensor(d, d, ident[:], ALU.add).then_inc(diag_added, 1)

            def low_w(t):
                dve.wait_ge(diag_added, t + 1)
                low(("w", t), w_lo[:, t, :], hi=w_hi[:, t, :].bitcast(f32))

            normalise(0)
            for k in range(STEPS + 1):
                if k + 1 < STEPS:
                    normalise(k + 1)
                if k == 0:
                    diag(4)
                if k < STEPS:
                    select(k)
                if k == 0:
                    low("a1", a1_lo[:].rearrange("p t c -> p (t c)"),
                        hi=a1_hi[:].rearrange("p t c -> p (t c)").bitcast(f32))
                    low_w(4)
                    diag(5)
                if k == 1:
                    low_w(5)
                    diag(6)
                    low_w(6)
                    diag(7)
                if k == 2:
                    low_w(7)
                if k >= 1 + NJ and (k - 1) % NJ == 0 and k < STEPS:
                    low_m((k - 1) // NJ - 1)
                if k >= 2 + NJ and (k - 2) % NJ == 0:
                    low_u((k - 2) // NJ - 1)

            def low_x(b):
                dve.wait_ge(x_hi_ready, b + 1)
                v.tensor_tensor(x_lo[:, b % 2, :, :].rearrange("p t c -> p (t c)"), x_raw[:, b % 2, :],
                                x_hi[:, b % 2, :, :].rearrange("p t c -> p (t c)").bitcast(f32),
                                ALU.subtract).then_inc(x_lo_ready, 1)

            def low_b(b):
                dve.wait_ge(b_hi_ready, b + 1)
                v.tensor_tensor(b_hl[P // 2:P, b % 2, :], b_raw[P // 2:P, :],
                                b_hl[P // 2:P, b % 2, :].bitcast(f32), ALU.subtract).then_inc(b_lo_ready, 1)

            low_x(0)
            low_m(NQ - 1)
            low_u(NQ - 1)
            low_b(0)
            for b in range(NB):
                if b + 1 < NB:
                    low_x(b + 1)
                dve.wait_ge(p_hi_ready, b + 1)
                for g in (1, 3):
                    s = slice(32 * g, 32 * g + 32)
                    v.tensor_tensor(p_hl[s, b % 2, :], ps_u[s, 0:TOK], p_hl[s, b % 2, :].bitcast(f32),
                                    ALU.subtract).then_inc(p_lo_ready, 1)
                if b + 1 < NB:
                    low_b(b + 1)
                for tt in range(TT):
                    dve.wait_ge(y_mm, 2 * (b * TT + tt) + 2)
                    if b:
                        dve.wait_ge(y_out[tt], 16 * b)
                    v.tensor_copy(y[:, tt, HB:D], acc[2 * tt + 1][:]).then_inc(y_dve, 1)

        @block.tensor
        def _(pe):
            t_ = nc.tensor

            def delta_product(k):
                q, j = k // NJ, k % NJ
                if k >= 2:
                    pe.wait_ge(delta_sb, k - 1)
                for t in range(OP):
                    rows = b0_hl[:, (j * OP + t) * P:(j * OP + t + 1) * P]
                    for n, a0 in enumerate((a0_hi, a0_lo)):
                        last = t_.matmul(ps_d[k % 2][:, t, :], rows, a0[:, q * QC:(q + 1) * QC],
                                         start=(n == 0), stop=(n == 1))
                last.then_inc(delta_mm, 1)

            def w_ready(t):
                if t >= 0:
                    pe.wait_ge(hi_made, AT[("w", t)] + 1)
                    low_wait(pe, ("w", t))

            def accumulate(k):
                q, j = k // NJ, k % NJ
                first, last_step = j == 0, j == NJ - 1
                pe.wait_ge(weff_hi_ready, k + 1)
                pe.wait_ge(weff_lo_ready, k + 1)
                if q == 0:
                    for t in range(OP):
                        w_ready(j * OP + t)
                for i in range(QI):
                    for h in range(2):
                        if first and q:
                            pe.wait_ge(m_hi_ready, 4 * (q - 1) + 2 * i + h + 1)
                            pe.wait_ge(m_lo_ready, 4 * (q - 1) + 2 * i + h + 1)
                        bank, cols = acc[2 * i + h][:], slice(h * HB, (h + 1) * HB)
                        for t in range(OP):
                            o = j * OP + t
                            hi = weff_hi[:, k % 2, t, i * P:(i + 1) * P]
                            lo = weff_lo[:, k % 2, t, i * P:(i + 1) * P]
                            t_.matmul(bank, hi, w_hi[:, o, cols], start=first and t == 0, stop=False)
                            t_.matmul(bank, hi, w_lo[:, o, cols], start=False, stop=False)
                            t_.matmul(bank, lo, w_hi[:, o, cols], start=False, stop=False)
                        if last_step:
                            t_.matmul(bank, ident_r[:], w_hi[:, q * QI + i, cols], start=False, stop=False)
                            t_.matmul(bank, ident_r[:], w_lo[:, q * QI + i, cols], start=False,
                                      stop=True).then_inc(m_acc, 1)
                if k == 0:
                    pe.wait_ge(lo_made_v, low_count("a1"))
                if first and q:
                    pe.wait_ge(ut_sb, q)
                for t in range(OP):
                    o = j * OP + t
                    hi, lo = weff_hi[:, k % 2, t, :], weff_lo[:, k % 2, t, :]
                    t_.matmul(ps_u[:, 0:QC], a1_hi[:, o, :], hi, start=first and t == 0, stop=False)
                    t_.matmul(ps_u[:, 0:QC], a1_lo[:, o, :], hi, start=False, stop=False)
                    last = t_.matmul(ps_u[:, 0:QC], a1_hi[:, o, :], lo, start=False, stop=False)
                last.then_inc(weff_used, 1)
                if last_step:
                    for i in range(QI):
                        for n, a1 in enumerate((a1_hi, a1_lo)):
                            last = t_.matmul(ps_u[:, i * P:(i + 1) * P], a1[:, q * QI + i, :], ident_r[:],
                                             start=False, stop=(i == QI - 1 and n == 1))
                    last.then_inc(ut_mm, 1)

            def turn_u(q):
                pe.wait_ge(ut_sb, q + 1)
                if q:
                    pe.wait_ge(u_lo_ready, q)
                for i in range(QI):
                    last = t_.transpose(ps_t[:, i * P:(i + 1) * P], ut[:, i * P:(i + 1) * P], ident[:])
                last.then_inc(u_back, 1)

            pe.wait_ge(hi_made, AT["a0"] + 1)
            pe.wait_ge(lo_made_v, low_count("a0"))
            delta_product(0)
            delta_product(1)
            delta_product(2)
            pe.wait_ge(ident_made, 2)
            for k in range(STEPS):
                if k + 3 < STEPS:
                    delta_product(k + 3)
                accumulate(k)
                if k >= NJ and k % NJ == 0:
                    turn_u(k // NJ - 1)
            turn_u(NQ - 1)

            for b in range(NB):
                s = b % 2
                pe.wait_ge(x_hi_ready, b + 1)
                pe.wait_ge(x_lo_ready, b + 1)
                pe.wait_ge(u_st_ready, 2 * (b + 1))
                if b:
                    pe.wait_ge(p_lo_ready, 2 * b)
                    pe.wait_ge(p_hi_ready, b)
                for i in range(DT):
                    ust = u_st[:, s, i, :, :, :].rearrange("p a c r -> p (a c r)")
                    for n, xx in enumerate((x_hi, x_lo)):
                        last = t_.matmul(ps_u[:, 0:TOK], ust, xx[:, s, i, :], start=(i == 0 and n == 0),
                                         stop=(i == DT - 1 and n == 1))
                last.then_inc(p_mm, 1)
                for tt in range(TT):
                    tok = slice(tt * P, (tt + 1) * P)
                    for h in range(2):
                        bank, cols = acc[2 * tt + h][:], slice(h * HB, (h + 1) * HB)
                        if b:
                            pe.wait_ge(y_dve if h else y_act, TT * (b - 1) + tt + 1)
                        else:
                            pe.wait_ge(m_hi_ready, 4 * NQ)
                            pe.wait_ge(m_lo_ready, 4 * NQ)
                        for i in range(DT):
                            t_.matmul(bank, x_hi[:, s, i, tok], m_hi[:, i, cols], start=(i == 0), stop=False)
                            t_.matmul(bank, x_hi[:, s, i, tok], m_lo[:, i, cols], start=False, stop=False)
                            t_.matmul(bank, x_lo[:, s, i, tok], m_hi[:, i, cols], start=False, stop=False)
                        pe.wait_ge(p_lo_ready, 2 * (b + 1))
                        pe.wait_ge(b_lo_ready, b + 1)
                        t_.matmul(bank, p_hl[:, s, tok], b_hl[:, s, cols], start=False,
                                  stop=True).then_inc(y_mm, 1)


def kernel(x, condB_codebook, itok_B_0_15, L0_cond_weight, L0_cond_scale_log, L0_cond_lora_A,
           L0_cond_lora_B, L1_cond_W, L1_cond_lora_A, L1_cond_lora_B):
    import numpy as np
    import concourse.bacc as bacc
    from concourse import mybir
    from concourse.bass_utils import run_bass_kernel_spmd

    B, S, D = x.shape
    T = D // P
    NA, _, R = L1_cond_lora_A.shape
    laid = {
        "xT": np.asarray(x).reshape(B, S, T, P).transpose(0, 3, 2, 1).reshape(B, P, T * S),
        "codebook": np.tile(np.asarray(condB_codebook)[None, :], (P, 1)),
        "adapter": np.asarray(itok_B_0_15).reshape(1, B),
        "weight": np.asarray(L0_cond_weight).reshape(T // 2, 2, P, D).transpose(0, 2, 1, 3),
        "scale_log": np.asarray(L0_cond_scale_log).reshape(T, P, -1).transpose(1, 0, 2).reshape(P, -1),
        "lora0_a": np.asarray(L0_cond_lora_A),
        "lora0_bT": np.asarray(L0_cond_lora_B).T,
        "w1": np.asarray(L1_cond_W),
        "lora1_a": np.asarray(L1_cond_lora_A).reshape(NA, T, P, R).transpose(0, 2, 1, 3),
        "lora1_b": np.asarray(L1_cond_lora_B),
    }
    nc = bacc.Bacc("TRN2", target_bir_lowering=False, num_devices=1)
    arrays, args = {}, []
    for name, a in laid.items():
        a = np.ascontiguousarray(a)
        arrays[name] = a
        args.append(nc.dram_tensor(name, a.shape, mybir.dt.from_np(a.dtype), kind="ExternalInput").ap())
    args.append(nc.dram_tensor("y_out", (B * S // P, P, D), mybir.dt.float32, kind="ExternalOutput").ap())
    two_layers(nc, *args)
    r = run_bass_kernel_spmd(nc, [arrays], core_ids=[0])
    return r.results[0]["y_out"].reshape(B, S, D)
```

```python
import concourse.bass as bass
from concourse import mybir
from contextlib import ExitStack

P = 128


def two_layers(nc, xT, codebook, adapter, weightT, scale_log, lora0_a, lora0_bT, w1, lora1_a, lora1_b, out):
    f32, f32r, i32, u8 = mybir.dt.float32, mybir.dt.float32r, mybir.dt.int32, mybir.dt.uint8
    ALU, ACT, AX = mybir.AluOpType, mybir.ActivationFunctionType, mybir.AxisListType

    NB = xT.shape[0]
    D = w1.shape[0]
    DT = D // P
    TOK = xT.shape[2] // DT
    TT = TOK // P
    NA, R1, _ = lora1_b.shape
    R0 = lora0_bT.shape[0]
    G = scale_log.shape[1] // DT
    HB = D // 2
    QI = 2
    QC = QI * P
    OP = 2
    NQ = DT // QI
    NJ = DT // OP
    STEPS = NQ * NJ
    SE = OP * QC
    NL = codebook.shape[1]
    assert 2 * R0 == P and NB * R1 == P and 8 * R1 == P and OP * QC == 512 and NL == 8 and G == DT

    ctx = ExitStack()

    def sem(name):
        return ctx.enter_context(nc.semaphore(name))

    def sb(stack, name, shape, dt):
        return stack.enter_context(nc.sbuf_tensor(name, shape, dt))

    with ctx:
        NS = DT + 3
        early = ExitStack()
        stage = sb(early, "stage", [P, NS, D], f32)
        early.close()
        m_hi = sb(ctx, "m_hi", [P, DT, D], f32r)
        m_lo = sb(ctx, "m_lo", [P, DT, D], f32r)
        u_hi = sb(ctx, "u_hi", [P, DT, NB * R1], f32r)
        u_lo = sb(ctx, "u_lo", [P, DT, NB * R1], f32r)

        one = ExitStack()
        a0_hi = sb(one, "a0_hi", [P, D], f32r)
        a0_lo = sb(one, "a0_lo", [P, D], f32r)
        b0_hl = sb(one, "b0_hl", [P, D], f32r)
        delta = sb(one, "delta", [P, 4, SE], f32)
        wraw = sb(one, "wraw", [P, 2, OP, QC], f32)
        norm = sb(one, "norm", [P, 3, SE], f32)
        quan = sb(one, "quan", [P, 3, SE], f32)
        upper = sb(one, "upper", [P, SE], f32)
        mask = sb(one, "mask", [P, 2, NL - 1, SE], u8)
        a1_hi = sb(one, "a1_hi", [P, DT, NB * R1], f32r)
        a1_lo = sb(one, "a1_lo", [P, DT, NB * R1], f32r)
        ident = sb(one, "ident", [P, P], f32)
        ident_r = sb(one, "ident_r", [P, P], f32r)
        cbn = sb(one, "cbn", [P, NL], f32)
        cbt = sb(one, "cbt", [P, NL], f32)
        cbmax = sb(one, "cbmax", [P, 2], f32)
        thr = sb(one, "thr", [P, NL - 1], f32)
        brk = sb(one, "brk", [P, NL - 1], f32)
        negbrk = sb(one, "negbrk", [P, NL - 1], f32)
        scale = sb(one, "scale", [P, DT * G], f32)
        rscale = sb(one, "rscale", [P, DT * G], f32)
        ex = sb(one, "ex", [P, 3, DT * G], f32)
        ki = sb(one, "ki", [P, 2, DT * G], i32)
        kb = sb(one, "kb", [P, 2, DT * G], i32)
        weff_hi = sb(one, "weff_hi", [P, 3, OP, QC], f32r)
        weff_lo = sb(one, "weff_lo", [P, 3, OP, QC], f32r)
        ut = sb(one, "ut", [P, QC], f32)
        w_hi = sb(one, "w_hi", [P, DT, D], f32r)
        w_lo = sb(one, "w_lo", [P, DT, D], f32r)
        one.close()

        x_raw = sb(ctx, "x_raw", [P, 2, DT * TOK], f32)
        b_raw = sb(ctx, "b_raw", [P, D], f32)
        x_hi = sb(ctx, "x_hi", [P, 2, DT, TOK], f32r)
        x_lo = sb(ctx, "x_lo", [P, 2, DT, TOK], f32r)
        b_hl = sb(ctx, "b_hl", [P, 2, D], f32r)
        u_st = sb(ctx, "u_st", [P, 2, DT, 4, 2, R1], f32r)
        p_hl = sb(ctx, "p_hl", [P, 2, TOK], f32r)
        y = sb(ctx, "y", [P, 2, D], f32)

        acc = [ctx.enter_context(nc.psum_tensor(f"acc{i}", [P, HB], f32)) for i in range(4)]
        ps_u = ctx.enter_context(nc.psum_tensor("ps_u", [P, HB], f32))
        ps_t = ctx.enter_context(nc.psum_tensor("ps_t", [P, HB], f32))
        ps_d = [ctx.enter_context(nc.psum_tensor(f"ps_d{i}", [P, OP, QC], f32)) for i in range(2)]

        codebook_in = sem("codebook_in")
        scale_log_in = sem("scale_log_in")
        staged_in = [sem(f"staged_in{i}") for i in range(NS)]
        weight_in = [sem(f"weight_in{i}") for i in range(2)]
        x_in = [sem(f"x_in{i}") for i in range(2)]
        b_in = sem("b_in")
        y_out = [sem(f"y_out{i}") for i in range(2)]
        ident_made = sem("ident_made")
        brk_ready = sem("brk_ready")
        scale_ready = sem("scale_ready")
        diag_added = sem("diag_added")
        hi_made = sem("hi_made")
        lo_made_v = sem("lo_made_v")
        lo_made_g = sem("lo_made_g")
        vchain = sem("vchain")
        gchain = sem("gchain")
        delta_mm = sem("delta_mm")
        delta_sb = sem("delta_sb")
        wsum = sem("wsum")
        norm_ready = sem("norm_ready")
        mask_ready = sem("mask_ready")
        select_done = sem("select_done")
        weff_ready = sem("weff_ready")
        weff_hi_ready = sem("weff_hi_ready")
        weff_lo_ready = sem("weff_lo_ready")
        weff_used = sem("weff_used")
        m_acc = sem("m_acc")
        m_hi_ready = sem("m_hi_ready")
        m_lo_ready = sem("m_lo_ready")
        ut_mm = sem("ut_mm")
        ut_sb = sem("ut_sb")
        u_back = sem("u_back")
        u_hi_ready = sem("u_hi_ready")
        u_lo_ready = sem("u_lo_ready")
        x_hi_ready = sem("x_hi_ready")
        x_lo_ready = sem("x_lo_ready")
        b_hi_ready = sem("b_hi_ready")
        b_lo_ready = sem("b_lo_ready")
        u_st_ready = sem("u_st_ready")
        p_mm = sem("p_mm")
        p_hi_ready = sem("p_hi_ready")
        p_lo_ready = sem("p_lo_ready")
        y_mm = sem("y_mm")
        y_act = sem("y_act")
        y_dve = sem("y_dve")

        block = ctx.enter_context(nc.Block())

        W = [("w", t) for t in range(DT)]
        STAGED = ["b0", "a0"] + W[:2] + ["a1"] + W[2:]
        BY_POOL = ["b0", W[0]]
        BY_VECTOR = ["a0", W[1], "a1"] + W[2:]
        AT = {item: n for n, item in enumerate(STAGED)}
        MASK_ORDER = [0, 4, 1, 5, 2, 6, 3]

        def staged(item):
            s = stage[:, AT[item], :]
            return s.rearrange("p (b t r) -> p t b r", b=NB, t=DT) if item == "a1" else s

        def by_adapter(t):
            return t[:].rearrange("p t (b r) -> p t b r", b=NB)

        def stage_wait(eng, item):
            eng.wait_ge(staged_in[AT[item]], 16 * {"b0": 2, "a0": 2, "a1": NB}.get(item, 1))

        def high_wait(eng, item):
            eng.wait_ge(hi_made, AT[item] + 1)

        def low_wait(eng, item):
            if item in BY_POOL:
                eng.wait_ge(lo_made_g, BY_POOL.index(item) + 1)
            else:
                eng.wait_ge(lo_made_v, BY_VECTOR.index(item) + 1)

        @block.sync
        def _(sp):
            def load(item):
                s, done = stage[:, AT[item], :], staged_in[AT[item]]
                if item in ("b0", "a0"):
                    src = {"b0": lora0_bT, "a0": lora0_a}[item]
                    sp.dma_start(s[0:R0, :], src).then_inc(done, 16)
                    sp.dma_start(s[R0:P, :], src).then_inc(done, 16)
                elif item == "a1":
                    s3 = s.rearrange("p (b c) -> p b c", b=NB)
                    for b in range(NB):
                        e = sp.value_load(adapter[0:1, b:b + 1], min_val=0, max_val=NA - 1)
                        sp.dma_start(s3[:, b, :], lora1_a[bass.ds(e, 1), :, :].rearrange("a p c -> (a p) c")
                                     ).then_inc(done, 16)
                else:
                    sp.dma_start(s, w1[item[1] * P:(item[1] + 1) * P, :]).then_inc(done, 16)

            def load_weight(k):
                q, j = k // NJ, k % NJ
                if k >= 2:
                    sp.wait_ge(wsum, k - 1)
                sp.dma_start(wraw[:, k % 2, :, :], weightT[j, :, :, q * QC:(q + 1) * QC]
                             ).then_inc(weight_in[k % 2], 16)

            sp.dma_start(ex[:, 0, :], scale_log).then_inc(scale_log_in, 16)
            sp.dma_start(cbt[:], codebook).then_inc(codebook_in, 16)
            load("b0")
            load("a0")
            load_weight(0)
            load_weight(1)
            for t in range(DT):
                load(("w", t))
            load("a1")
            for k in range(2, STEPS):
                load_weight(k)

            def load_x(b, slot):
                sp.dma_start(x_raw[:, slot, :], xT[bass.ds(b, 1), :, :].rearrange(
                    "b p c -> (b p) c")).then_inc(x_in[slot], 16)

            def load_b(b):
                e = sp.value_load(adapter[0:1, bass.ds(b, 1)], min_val=0, max_val=NA - 1)
                src = lora1_b[bass.ds(e, 1), :, :].rearrange("a r n -> (a r) n")
                for g in range(P // R1):
                    sp.dma_start(b_raw[g * R1:(g + 1) * R1, :], src).then_inc(b_in, 16)

            def store(b, tt, done):
                sp.wait_ge(y_act, done)
                sp.wait_ge(y_dve, done)
                sp.dma_start(out[bass.ds(b * TT + tt, 1), :, :].rearrange("t p n -> (t p) n"),
                             y[:, tt, :]).then_inc(y_out[tt], 16)

            sp.wait_ge(delta_mm, STEPS)
            sp.wait_ge(weff_ready, STEPS)
            load_x(0, 0)
            sp.wait_ge(weff_lo_ready, STEPS)
            sp.wait_ge(weff_hi_ready, STEPS)
            load_x(1, 1)
            load_b(0)
            for b in range(NB):
                if b + 1 < NB:
                    sp.wait_ge(b_hi_ready, b + 1)
                    sp.wait_ge(b_lo_ready, b + 1)
                    load_b(b + 1)
                if b + 2 < NB:
                    sp.wait_ge(x_hi_ready, b + 1)
                    sp.wait_ge(x_lo_ready, b + 1)
                    load_x(b + 2, b % 2)
                for tt in range(TT):
                    store(b, tt, b * TT + tt + 1)
            for tt in range(TT):
                sp.wait_ge(y_out[tt], 16 * NB)

        @block.gpsimd
        def _(pool):
            g = nc.gpsimd
            chain = [0]

            def link(ins):
                chain[0] += 1
                ins.then_inc(gchain, 1)
                pool.wait_ge(gchain, chain[0])

            link(g.memset(ident[:], 0.0))
            g.affine_select(out=ident[:], in_=ident[:], compare_op=ALU.not_equal, fill=1.0, base=0,
                            pattern=[[-1, P]], channel_multiplier=1).then_inc(ident_made, 1)
            pool.wait_ge(ident_made, 1)

            def diag(t):
                stage_wait(pool, ("w", t))
                d = stage[:, AT[("w", t)], t * P:(t + 1) * P]
                g.tensor_tensor(d, d, ident[:], ALU.add).then_inc(diag_added, 1)

            def low(item, dst, hi, rows=slice(0, P)):
                high_wait(pool, item)
                g.tensor_tensor(dst, stage[rows, AT[item], :], hi.bitcast(f32), ALU.subtract).then_inc(lo_made_g, 1)

            low("b0", b0_hl[R0:P, :], b0_hl[R0:P, :], slice(R0, P))
            low_wait(pool, "b0")
            diag(0)
            low(W[0], w_lo[:, 0, :], w_hi[:, 0, :])
            for t in range(1, DT):
                diag(t)

            def sc(k):
                q, j = k // NJ, k % NJ
                s = scale[:].rearrange("p (t g) -> p t g", g=G)[:, j * OP:(j + 1) * OP, q * QI:(q + 1) * QI]
                return s.unsqueeze(3).broadcast_to([P, OP, QI, P])

            def low_weff(k):
                pool.wait_ge(weff_hi_ready, k + 1)
                if k >= 3:
                    pool.wait_ge(weff_used, k - 2)
                g.tensor_tensor(weff_lo[:, k % 3, :, :].rearrange("p t c -> p (t c)"), quan[:, k % 3, :],
                                weff_hi[:, k % 3, :, :].rearrange("p t c -> p (t c)").bitcast(f32),
                                ALU.subtract).then_inc(weff_lo_ready, 1)

            def dequantise(k):
                v = quan[:, k % 3, :]
                v4 = v.rearrange("p (t g c) -> p t g c", t=OP, g=QI)
                pool.wait_ge(select_done, 9 * (k + 1))
                link(g.tensor_tensor(v, v, norm[:, k % 3, :], ALU.subtract))
                link(g.tensor_tensor(v, v, norm[:, k % 3, :], ALU.add))
                link(g.tensor_tensor(v4, v4, sc(k), ALU.mult))
                pool.wait_ge(delta_sb, k + 1)
                g.tensor_tensor(v, v, delta[:, k % 4, :], ALU.add).then_inc(weff_ready, 1)

            pool.wait_ge(scale_ready, 1)
            for k in range(STEPS):
                if k:
                    low_weff(k - 1)
                dequantise(k)
            low_weff(STEPS - 1)

        @block.scalar
        def _(act):
            a = nc.scalar

            def high(item, dst):
                stage_wait(act, item)
                if item[0] == "w":
                    act.wait_ge(diag_added, item[1] + 1)
                a.activation(dst, staged(item), ACT.Copy).then_inc(hi_made, 1)

            def copy_delta(k):
                act.wait_ge(delta_mm, k + 1)
                if k >= 4:
                    act.wait_ge(weff_ready, k - 3)
                a.activation(delta[:, k % 4, :], ps_d[k % 2][:].rearrange("p t c -> p (t c)"), ACT.Copy,
                             scale=0.5).then_inc(delta_sb, 1)

            def masks(k):
                act.wait_ge(norm_ready, k + 1)
                if k >= 2:
                    act.wait_ge(select_done, 9 * (k - 1))
                for i in MASK_ORDER:
                    a.activation(mask[:, k % 2, i, :], norm[:, k % 3, :], ACT.Sign,
                                 bias=negbrk[:, i:i + 1]).then_inc(mask_ready, 1)

            def high_weff(k):
                act.wait_ge(weff_ready, k + 1)
                if k >= 3:
                    act.wait_ge(weff_used, k - 2)
                    act.wait_ge(weff_lo_ready, k - 2)
                a.activation(weff_hi[:, k % 3, :, :].rearrange("p t c -> p (t c)"), quan[:, k % 3, :],
                             ACT.Copy).then_inc(weff_hi_ready, 1)

            def high_m(q, i):
                for h in range(2):
                    act.wait_ge(m_acc, 4 * q + 2 * i + h + 1)
                    a.activation(m_hi[:, q * QI + i, h * HB:(h + 1) * HB], acc[2 * i + h][:],
                                 ACT.Copy).then_inc(m_hi_ready, 1)

            def take_ut(q):
                act.wait_ge(ut_mm, q + 1)
                if q:
                    act.wait_ge(u_back, q)
                a.activation(ut[:], ps_u[:, 0:QC], ACT.Copy).then_inc(ut_sb, 1)

            def high_u(q):
                act.wait_ge(u_back, q + 1)
                a.activation(u_hi[:, q * QI:(q + 1) * QI, :],
                             ps_t[:, 0:QC].rearrange("p (t c) -> p t c", t=QI), ACT.Copy).then_inc(u_hi_ready, 1)

            high("b0", b0_hl[:])
            high("a0", a0_hi[:])
            act.wait_ge(ident_made, 1)
            a.activation(ident_r[:], ident[:], ACT.Copy).then_inc(ident_made, 1)
            copy_delta(0)
            high(("w", 0), w_hi[:, 0, :])
            act.wait_ge(brk_ready, 1)
            for k in range(STEPS + 1):
                if k + 1 < STEPS:
                    copy_delta(k + 1)
                ended = k >= 3 + NJ and (k - 3) % NJ == 0 and k < STEPS
                if ended:
                    high_m((k - 3) // NJ - 1, 0)
                    high_m((k - 3) // NJ - 1, 1)
                if k < STEPS:
                    masks(k)
                if k >= 1:
                    high_weff(k - 1)
                if ended:
                    take_ut((k - 3) // NJ - 1)
                if k >= NJ and k % NJ == 0 and k // NJ >= 2:
                    high_u(k // NJ - 2)
                if k == 1:
                    high("a1", by_adapter(a1_hi))
                for t in range(2 * k, 2 * k + 2) if k < NJ else ():
                    if t:
                        high(W[t], w_hi[:, t, :])

            def high_x(b):
                act.wait_ge(x_in[b % 2], 16 * (b // 2 + 1))
                if b >= 2:
                    act.wait_ge(y_mm, 2 * TT * (b - 1))
                a.activation(x_hi[:, b % 2, :, :].rearrange("p t c -> p (t c)"), x_raw[:, b % 2, :],
                             ACT.Copy).then_inc(x_hi_ready, 1)

            def high_b(b):
                act.wait_ge(b_in, 16 * (P // R1) * (b + 1))
                if b >= 2:
                    act.wait_ge(y_mm, 2 * TT * (b - 1))
                a.activation(b_hl[:, b % 2, :], b_raw[:], ACT.Copy).then_inc(b_hi_ready, 1)

            def stack_u(b):
                if b >= 2:
                    act.wait_ge(p_mm, b - 1)
                for c, u in enumerate((u_hi, u_lo)):
                    src = u[:, :, b * R1:(b + 1) * R1].bitcast(f32).unsqueeze(2).broadcast_to([P, DT, 4, R1])
                    a.activation(u_st[:, b % 2, :, :, c, :], src, ACT.Copy).then_inc(u_st_ready, 1)

            act.wait_ge(weff_lo_ready, STEPS)
            high_x(0)
            high_m(NQ - 1, 0)
            high_m(NQ - 1, 1)
            take_ut(NQ - 1)
            high_u(NQ - 1)
            act.wait_ge(u_hi_ready, NQ)
            act.wait_ge(u_lo_ready, NQ)
            stack_u(0)
            high_b(0)
            for b in range(NB):
                if b + 1 < NB:
                    high_x(b + 1)
                    stack_u(b + 1)
                act.wait_ge(p_mm, b + 1)
                if b >= 2:
                    act.wait_ge(y_mm, 2 * TT * (b - 1))
                a.activation(p_hl[:, b % 2, :], ps_u[:, 0:TOK], ACT.Copy).then_inc(p_hi_ready, 1)
                if b + 1 < NB:
                    high_b(b + 1)
                for tt in range(TT):
                    act.wait_ge(y_mm, 2 * (b * TT + tt) + 1)
                    if b:
                        act.wait_ge(y_out[tt], 16 * b)
                    a.activation(y[:, tt, 0:HB], acc[2 * tt][:], ACT.Copy).then_inc(y_act, 1)

        @block.vector
        def _(dve):
            v = nc.vector
            chain = [0]

            def low(item, dst, hi):
                high_wait(dve, item)
                v.tensor_tensor(dst, staged(item), hi.bitcast(f32), ALU.subtract).then_inc(lo_made_v, 1)

            def turn(ins):
                chain[0] += 1
                ins.then_inc(vchain, 1)
                if chain[0] > 1:
                    dve.wait_ge(vchain, chain[0] - 1)

            x_, r_, p_ = ex[:, 0, :], ex[:, 1, :], ex[:, 2, :]

            def horner(c):
                return v.scalar_tensor_tensor(out=p_, in0=p_, scalar=c, in1=r_, op0=ALU.add, op1=ALU.mult)

            dve.wait_ge(scale_log_in, 16)
            dve.wait_ge(codebook_in, 16)
            turn(v.tensor_scalar(x_, x_, -104.0, 89.5, ALU.max, ALU.min))
            turn(v.tensor_scalar(cbn[:], cbt[:], -1.0, None, ALU.mult))
            turn(v.tensor_scalar(ki[:, 1, :], x_, 1.4426950408889634, None, ALU.mult))
            turn(v.tensor_tensor(cbn[:], cbn[:], cbt[:], ALU.max))
            turn(v.tensor_copy(p_, ki[:, 1, :]))
            turn(v.reduce_max(cbmax[:, 0:1], cbn[:], AX.X))
            turn(v.scalar_tensor_tensor(out=r_, in0=p_, scalar=-0.693359375, in1=x_, op0=ALU.mult, op1=ALU.add))
            turn(v.tensor_scalar(cbmax[:, 0:1], cbmax[:, 0:1], 1e-8, None, ALU.max))
            turn(v.scalar_tensor_tensor(out=r_, in0=p_, scalar=2.12194440e-4, in1=r_, op0=ALU.mult, op1=ALU.add))
            turn(v.reciprocal(cbmax[:, 1:2], cbmax[:, 0:1]))
            turn(v.tensor_scalar(p_, r_, 1.0 / 5040, None, ALU.mult))
            turn(v.tensor_scalar(cbn[:], cbt[:], cbmax[:, 1:2], None, ALU.mult))
            turn(horner(1.0 / 720))
            turn(v.tensor_tensor(thr[:], cbn[:, 0:NL - 1], cbn[:, 1:NL], ALU.add))
            turn(horner(1.0 / 120))
            turn(v.tensor_scalar(thr[:], thr[:], 0.5, None, ALU.mult))
            turn(horner(1.0 / 24))
            turn(v.tensor_copy(brk[:, 3:4], thr[:, 3:4]))
            turn(horner(1.0 / 6))
            turn(v.tensor_tensor(brk[:, 1:2], thr[:, 1:2], brk[:, 3:4], ALU.min))
            turn(horner(0.5))
            turn(v.tensor_tensor(brk[:, 5:6], thr[:, 5:6], brk[:, 3:4], ALU.max))
            turn(horner(1.0))
            turn(v.tensor_scalar(ki[:, 0, :], ki[:, 1, :], 1, None, ALU.arith_shift_right))
            turn(v.tensor_scalar(p_, p_, 1.0, None, ALU.add))
            turn(v.tensor_tensor(ki[:, 1, :], ki[:, 1, :], ki[:, 0, :], ALU.subtract))
            turn(v.tensor_tensor(brk[:, 2:5:2], thr[:, 2:5:2], brk[:, 1:4:2], ALU.max))
            turn(v.tensor_scalar(kb[:], ki[:], 127.0, None, ALU.add))
            turn(v.tensor_tensor(brk[:, 2:5:2], brk[:, 2:5:2], brk[:, 3:6:2], ALU.min))
            turn(v.tensor_scalar(kb[:], kb[:], 23, None, ALU.logical_shift_left))
            turn(v.tensor_tensor(brk[:, 0:1], thr[:, 0:1], brk[:, 1:2], ALU.min))
            turn(v.tensor_tensor(p_, p_, kb[:, 0, :].bitcast(f32), ALU.mult))
            turn(v.tensor_tensor(brk[:, 6:7], thr[:, 6:7], brk[:, 5:6], ALU.max))
            turn(v.tensor_tensor(scale[:], p_, kb[:, 1, :].bitcast(f32), ALU.mult))
            v.tensor_scalar(negbrk[:], brk[:], -1.0, None, ALU.mult).then_inc(brk_ready, 1)
            dve.wait_ge(vchain, chain[0])
            v.reciprocal(rscale[:], scale[:]).then_inc(scale_ready, 1)
            low("a0", a0_lo[:], a0_hi[:])
            dve.wait_ge(scale_ready, 1)

            def normalise(k):
                q, j = k // NJ, k % NJ
                dve.wait_ge(delta_sb, k + 1)
                dve.wait_ge(weight_in[k % 2], 16 * (k // 2 + 1))
                if k >= 3:
                    dve.wait_ge(weff_ready, k - 2)
                n = norm[:, k % 3, :]
                v.tensor_tensor(n, delta[:, k % 4, :], wraw[:, k % 2, :, :].rearrange("p t c -> p (t c)"),
                                ALU.add).then_inc(wsum, 1)
                dve.wait_ge(wsum, k + 1)
                n4 = n.rearrange("p (t g c) -> p t g c", t=OP, g=QI)
                r = rscale[:].rearrange("p (t g) -> p t g", g=G)[:, j * OP:(j + 1) * OP, q * QI:(q + 1) * QI]
                v.tensor_tensor(n4, n4, r.unsqueeze(3).broadcast_to([P, OP, QI, P]),
                                ALU.mult).then_inc(norm_ready, 1)

            def select(k):
                lower = quan[:, k % 3, :]
                if k >= 3:
                    dve.wait_ge(weff_lo_ready, k - 2)
                    dve.wait_ge(weff_hi_ready, k - 2)
                done = 9 * k
                if k:
                    dve.wait_ge(select_done, done)
                v.tensor_copy(lower, cbn[:, 0:1].broadcast_to([P, SE])).then_inc(select_done, 1)
                v.tensor_copy(upper[:], cbn[:, 4:5].broadcast_to([P, SE])).then_inc(select_done, 1)
                done += 2
                for n, i in enumerate(MASK_ORDER):
                    dve.wait_ge(mask_ready, 7 * k + n + 1)
                    dve.wait_ge(select_done, done + n - 1 + (i == 3))
                    dst = upper[:] if i > 3 else lower
                    data = upper[:] if i == 3 else cbn[:, i + 1:i + 2].broadcast_to([P, SE])
                    v.copy_predicated(dst, mask[:, k % 2, i, :], data).then_inc(select_done, 1)

            def low_m(q, i):
                for h in range(2):
                    dve.wait_ge(m_hi_ready, 4 * q + 2 * i + h + 1)
                    s = slice(h * HB, (h + 1) * HB)
                    v.tensor_tensor(m_lo[:, q * QI + i, s], acc[2 * i + h][:],
                                    m_hi[:, q * QI + i, s].bitcast(f32), ALU.subtract).then_inc(m_lo_ready, 1)

            def low_u(q):
                dve.wait_ge(u_hi_ready, q + 1)
                v.tensor_tensor(u_lo[:, q * QI:(q + 1) * QI, :],
                                ps_t[:, 0:QC].rearrange("p (t c) -> p t c", t=QI),
                                u_hi[:, q * QI:(q + 1) * QI, :].bitcast(f32), ALU.subtract).then_inc(u_lo_ready, 1)

            def low_w(t):
                low(("w", t), w_lo[:, t, :], w_hi[:, t, :])

            normalise(0)
            for k in range(STEPS):
                if k + 1 < STEPS:
                    normalise(k + 1)
                ended = k >= 2 + NJ and (k - 2) % NJ == 0
                select(k)
                if ended:
                    low_m((k - 2) // NJ - 1, 0)
                    low_m((k - 2) // NJ - 1, 1)
                if k == 1:
                    low("a1", by_adapter(a1_lo), by_adapter(a1_hi))
                for t in range(2 * k, 2 * k + 2) if k < NJ else ():
                    if t:
                        low_w(t)
                if k >= NJ and k % NJ == 0 and k // NJ >= 2:
                    low_u(k // NJ - 2)

            def low_x(b):
                dve.wait_ge(x_hi_ready, b + 1)
                v.tensor_tensor(x_lo[:, b % 2, :, :].rearrange("p t c -> p (t c)"), x_raw[:, b % 2, :],
                                x_hi[:, b % 2, :, :].rearrange("p t c -> p (t c)").bitcast(f32),
                                ALU.subtract).then_inc(x_lo_ready, 1)

            def low_b(b):
                dve.wait_ge(b_hi_ready, b + 1)
                v.tensor_tensor(b_hl[P // 2:P, b % 2, :], b_raw[P // 2:P, :],
                                b_hl[P // 2:P, b % 2, :].bitcast(f32), ALU.subtract).then_inc(b_lo_ready, 1)

            low_u(NQ - 2)
            low_x(0)
            low_m(NQ - 1, 0)
            low_m(NQ - 1, 1)
            low_u(NQ - 1)
            low_b(0)
            for b in range(NB):
                if b + 1 < NB:
                    low_x(b + 1)
                dve.wait_ge(p_hi_ready, b + 1)
                for g in (1, 3):
                    s = slice(32 * g, 32 * g + 32)
                    v.tensor_tensor(p_hl[s, b % 2, :], ps_u[s, 0:TOK], p_hl[s, b % 2, :].bitcast(f32),
                                    ALU.subtract).then_inc(p_lo_ready, 1)
                if b + 1 < NB:
                    low_b(b + 1)
                for tt in range(TT):
                    dve.wait_ge(y_mm, 2 * (b * TT + tt) + 2)
                    if b:
                        dve.wait_ge(y_out[tt], 16 * b)
                    v.tensor_copy(y[:, tt, HB:D], acc[2 * tt + 1][:]).then_inc(y_dve, 1)

        @block.tensor
        def _(pe):
            t_ = nc.tensor

            def delta_product(k):
                q, j = k // NJ, k % NJ
                if k >= 2:
                    pe.wait_ge(delta_sb, k - 1)
                for t in range(OP):
                    rows = b0_hl[:, (j * OP + t) * P:(j * OP + t + 1) * P]
                    for n, a0 in enumerate((a0_hi, a0_lo)):
                        last = t_.matmul(ps_d[k % 2][:, t, :], rows, a0[:, q * QC:(q + 1) * QC],
                                         start=(n == 0), stop=(n == 1))
                last.then_inc(delta_mm, 1)

            def w_ready(t):
                high_wait(pe, ("w", t))
                low_wait(pe, ("w", t))

            def accumulate(k):
                q, j = k // NJ, k % NJ
                first, last_step = j == 0, j == NJ - 1
                pe.wait_ge(weff_hi_ready, k + 1)
                pe.wait_ge(weff_lo_ready, k + 1)
                if q == 0:
                    for t in range(OP):
                        w_ready(j * OP + t)
                for i in range(QI):
                    for h in range(2):
                        if first and q:
                            pe.wait_ge(m_hi_ready, 4 * (q - 1) + 2 * i + h + 1)
                            pe.wait_ge(m_lo_ready, 4 * (q - 1) + 2 * i + h + 1)
                        bank, cols = acc[2 * i + h][:], slice(h * HB, (h + 1) * HB)
                        for t in range(OP):
                            o = j * OP + t
                            hi = weff_hi[:, k % 3, t, i * P:(i + 1) * P]
                            lo = weff_lo[:, k % 3, t, i * P:(i + 1) * P]
                            t_.matmul(bank, hi, w_hi[:, o, cols], start=first and t == 0, stop=False)
                            t_.matmul(bank, hi, w_lo[:, o, cols], start=False, stop=False)
                            t_.matmul(bank, lo, w_hi[:, o, cols], start=False, stop=False)
                        if last_step:
                            t_.matmul(bank, ident_r[:], w_hi[:, q * QI + i, cols], start=False, stop=False)
                            t_.matmul(bank, ident_r[:], w_lo[:, q * QI + i, cols], start=False,
                                      stop=True).then_inc(m_acc, 1)
                if k == 0:
                    low_wait(pe, "a1")
                if first and q:
                    pe.wait_ge(ut_sb, q)
                for t in range(OP):
                    o = j * OP + t
                    hi, lo = weff_hi[:, k % 3, t, :], weff_lo[:, k % 3, t, :]
                    t_.matmul(ps_u[:, 0:QC], a1_hi[:, o, :], hi, start=first and t == 0, stop=False)
                    t_.matmul(ps_u[:, 0:QC], a1_lo[:, o, :], hi, start=False, stop=False)
                    last = t_.matmul(ps_u[:, 0:QC], a1_hi[:, o, :], lo, start=False, stop=False)
                last.then_inc(weff_used, 1)
                if last_step:
                    for i in range(QI):
                        for n, a1 in enumerate((a1_hi, a1_lo)):
                            last = t_.matmul(ps_u[:, i * P:(i + 1) * P], a1[:, q * QI + i, :], ident_r[:],
                                             start=False, stop=(i == QI - 1 and n == 1))
                    last.then_inc(ut_mm, 1)

            def turn_u(q):
                pe.wait_ge(ut_sb, q + 1)
                if q:
                    pe.wait_ge(u_lo_ready, q)
                for i in range(QI):
                    last = t_.transpose(ps_t[:, i * P:(i + 1) * P], ut[:, i * P:(i + 1) * P], ident[:])
                last.then_inc(u_back, 1)

            high_wait(pe, "a0")
            low_wait(pe, "a0")
            low_wait(pe, "b0")
            delta_product(0)
            delta_product(1)
            delta_product(2)
            delta_product(3)
            pe.wait_ge(ident_made, 2)
            for k in range(STEPS):
                if k + 4 < STEPS:
                    delta_product(k + 4)
                accumulate(k)
                if k >= NJ and k % NJ == 0:
                    turn_u(k // NJ - 1)
            turn_u(NQ - 1)

            for b in range(NB):
                s = b % 2
                pe.wait_ge(x_hi_ready, b + 1)
                pe.wait_ge(x_lo_ready, b + 1)
                pe.wait_ge(u_st_ready, 2 * (b + 1))
                if b:
                    pe.wait_ge(p_lo_ready, 2 * b)
                    pe.wait_ge(p_hi_ready, b)
                for i in range(DT):
                    ust = u_st[:, s, i, :, :, :].rearrange("p a c r -> p (a c r)")
                    for n, xx in enumerate((x_hi, x_lo)):
                        last = t_.matmul(ps_u[:, 0:TOK], ust, xx[:, s, i, :], start=(i == 0 and n == 0),
                                         stop=(i == DT - 1 and n == 1))
                last.then_inc(p_mm, 1)
                for tt in range(TT):
                    tok = slice(tt * P, (tt + 1) * P)
                    for h in range(2):
                        bank, cols = acc[2 * tt + h][:], slice(h * HB, (h + 1) * HB)
                        if b:
                            pe.wait_ge(y_dve if h else y_act, TT * (b - 1) + tt + 1)
                        else:
                            pe.wait_ge(m_hi_ready, 4 * NQ)
                            pe.wait_ge(m_lo_ready, 4 * NQ)
                        for i in range(DT):
                            t_.matmul(bank, x_hi[:, s, i, tok], m_hi[:, i, cols], start=(i == 0), stop=False)
                            t_.matmul(bank, x_hi[:, s, i, tok], m_lo[:, i, cols], start=False, stop=False)
                            t_.matmul(bank, x_lo[:, s, i, tok], m_hi[:, i, cols], start=False, stop=False)
                        pe.wait_ge(p_lo_ready, 2 * (b + 1))
                        pe.wait_ge(b_lo_ready, b + 1)
                        t_.matmul(bank, p_hl[:, s, tok], b_hl[:, s, cols], start=False,
                                  stop=True).then_inc(y_mm, 1)


def kernel(x, condB_codebook, itok_B_0_15, L0_cond_weight, L0_cond_scale_log, L0_cond_lora_A,
           L0_cond_lora_B, L1_cond_W, L1_cond_lora_A, L1_cond_lora_B):
    import numpy as np
    import concourse.bacc as bacc
    from concourse import mybir
    from concourse.bass_utils import run_bass_kernel_spmd

    B, S, D = x.shape
    T = D // P
    NA, _, R = L1_cond_lora_A.shape
    laid = {
        "xT": np.asarray(x).reshape(B, S, T, P).transpose(0, 3, 2, 1).reshape(B, P, T * S),
        "codebook": np.tile(np.asarray(condB_codebook)[None, :], (P, 1)),
        "adapter": np.asarray(itok_B_0_15).reshape(1, B),
        "weight": np.asarray(L0_cond_weight).reshape(T // 2, 2, P, D).transpose(0, 2, 1, 3),
        "scale_log": np.asarray(L0_cond_scale_log).reshape(T, P, -1).transpose(1, 0, 2).reshape(P, -1),
        "lora0_a": np.asarray(L0_cond_lora_A),
        "lora0_bT": np.asarray(L0_cond_lora_B).T,
        "w1": np.asarray(L1_cond_W),
        "lora1_a": np.asarray(L1_cond_lora_A).reshape(NA, T, P, R).transpose(0, 2, 1, 3).reshape(NA, P, T * R),
        "lora1_b": np.asarray(L1_cond_lora_B),
    }
    nc = bacc.Bacc("TRN2", target_bir_lowering=False, num_devices=1)
    arrays, args = {}, []
    for name, a in laid.items():
        a = np.ascontiguousarray(a)
        arrays[name] = a
        args.append(nc.dram_tensor(name, a.shape, mybir.dt.from_np(a.dtype), kind="ExternalInput").ap())
    args.append(nc.dram_tensor("y_out", (B * S // P, P, D), mybir.dt.float32, kind="ExternalOutput").ap())
    two_layers(nc, *args)
    r = run_bass_kernel_spmd(nc, [arrays], core_ids=[0])
    return r.results[0]["y_out"].reshape(B, S, D)
```

```python
import concourse.bass as bass
from concourse import mybir
from contextlib import ExitStack

P = 128


def two_layers(nc, xT, codebook, adapter, weightT, scale_log, lora0_a, lora0_bT, w1, lora1_a, lora1_b, out):
    f32, f32r, i32, u8 = mybir.dt.float32, mybir.dt.float32r, mybir.dt.int32, mybir.dt.uint8
    ALU, ACT, AX = mybir.AluOpType, mybir.ActivationFunctionType, mybir.AxisListType

    NB = xT.shape[0]
    D = w1.shape[0]
    DT = D // P
    TOK = xT.shape[2] // DT
    TT = TOK // P
    NA, R1, _ = lora1_b.shape
    R0 = lora0_bT.shape[0] // 2
    G = scale_log.shape[1] // DT
    HB = D // 2
    QI = 2
    QC = QI * P
    OP = 2
    NQ = DT // QI
    NJ = DT // OP
    STEPS = NQ * NJ
    SE = OP * QC
    NL = codebook.shape[1]
    assert 2 * R0 == P and NB * R1 == P and 8 * R1 == P and OP * QC == 512 and NL == 8 and G == DT

    ctx = ExitStack()

    def sem(name):
        return ctx.enter_context(nc.semaphore(name))

    def sb(stack, name, shape, dt):
        return stack.enter_context(nc.sbuf_tensor(name, shape, dt))

    with ctx:
        ids = sb(ctx, "ids", [1, NB], i32)
        NS = DT + 3
        early = ExitStack()
        stage = sb(early, "stage", [P, NS, D], f32)
        early.close()
        whole = ExitStack()
        sb(whole, "below_whole", [P, DT, D], f32)
        m_whole = sb(whole, "m_whole", [P, DT, D], f32)
        whole.close()
        m_hi = sb(ctx, "m_hi", [P, DT, D], f32r)
        m_lo = sb(ctx, "m_lo", [P, DT, D], f32r)
        u_hi = sb(ctx, "u_hi", [P, DT, NB * R1], f32r)
        u_lo = sb(ctx, "u_lo", [P, DT, NB * R1], f32r)

        one = ExitStack()
        a0_hi = sb(one, "a0_hi", [P, D], f32r)
        a0_lo = sb(one, "a0_lo", [P, D], f32r)
        b0_hl = sb(one, "b0_hl", [P, D], f32r)
        delta = sb(one, "delta", [P, 4, SE], f32)
        wraw = sb(one, "wraw", [P, 2, OP, QC], f32)
        norm = sb(one, "norm", [P, 3, SE], f32)
        quan = sb(one, "quan", [P, 3, SE], f32)
        upper = sb(one, "upper", [P, SE], f32)
        mask = sb(one, "mask", [P, 2, NL - 1, SE], u8)
        a1_hi = sb(one, "a1_hi", [P, DT, NB * R1], f32r)
        a1_lo = sb(one, "a1_lo", [P, DT, NB * R1], f32r)
        ident = sb(one, "ident", [P, P], f32)
        cbn = sb(one, "cbn", [P, NL], f32)
        cbt = sb(one, "cbt", [P, NL], f32)
        cbmax = sb(one, "cbmax", [P, 2], f32)
        thr = sb(one, "thr", [P, NL - 1], f32)
        brk = sb(one, "brk", [P, NL - 1], f32)
        negbrk = sb(one, "negbrk", [P, NL - 1], f32)
        scale = sb(one, "scale", [P, DT * G], f32)
        rscale = sb(one, "rscale", [P, DT * G], f32)
        ex = sb(one, "ex", [P, 3, DT * G], f32)
        ki = sb(one, "ki", [P, 2, DT * G], i32)
        kb = sb(one, "kb", [P, 2, DT * G], i32)
        weff_hi = sb(one, "weff_hi", [P, 3, OP, QC], f32r)
        weff_lo = sb(one, "weff_lo", [P, 3, OP, QC], f32r)
        ut = sb(one, "ut", [P, QC], f32)
        w_hi = sb(one, "w_hi", [P, DT, D], f32r)
        w_lo = sb(one, "w_lo", [P, DT, D], f32r)
        one.close()

        x_raw = sb(ctx, "x_raw", [P, 2, DT * TOK], f32)
        b_raw = sb(ctx, "b_raw", [P, D], f32)
        x_hi = sb(ctx, "x_hi", [P, 2, DT, TOK], f32r)
        x_lo = sb(ctx, "x_lo", [P, 2, DT, TOK], f32r)
        b_hl = sb(ctx, "b_hl", [P, 2, D], f32r)
        u_st = sb(ctx, "u_st", [P, 2, DT, 4, 2, R1], f32r)
        p_hl = sb(ctx, "p_hl", [P, 2, TOK], f32r)
        y = sb(ctx, "y", [P, 2, D], f32)

        acc = [ctx.enter_context(nc.psum_tensor(f"acc{i}", [P, HB], f32)) for i in range(4)]
        ps_u = ctx.enter_context(nc.psum_tensor("ps_u", [P, HB], f32))
        ps_t = ctx.enter_context(nc.psum_tensor("ps_t", [P, HB], f32))
        ps_d = [ctx.enter_context(nc.psum_tensor(f"ps_d{i}", [P, OP, QC], f32)) for i in range(2)]

        codebook_in = sem("codebook_in")
        scale_log_in = sem("scale_log_in")
        ids_in = sem("ids_in")
        staged_in = [sem(f"staged_in{i}") for i in range(NS)]
        rest_in = [sem(f"rest_in{i}") for i in range(2)]
        weight_in = [sem(f"weight_in{i}") for i in range(2)]
        x_in = [sem(f"x_in{i}") for i in range(2)]
        b_in = sem("b_in")
        y_out = [sem(f"y_out{i}") for i in range(2)]
        ident_made = sem("ident_made")
        brk_ready = sem("brk_ready")
        scale_ready = sem("scale_ready")
        diag_added = sem("diag_added")
        hi_made = sem("hi_made")
        lo_made_v = sem("lo_made_v")
        lo_made_g = sem("lo_made_g")
        vchain = sem("vchain")
        last_chain = sem("last_chain")
        gchain = sem("gchain")
        delta_mm = sem("delta_mm")
        delta_sb = sem("delta_sb")
        wsum = sem("wsum")
        norm_ready = sem("norm_ready")
        mask_ready = sem("mask_ready")
        upper_started = sem("upper_started")
        select_done = sem("select_done")
        weff_ready = sem("weff_ready")
        weff_ready_v = sem("weff_ready_v")
        weff_hi_ready = sem("weff_hi_ready")
        weff_lo_ready = sem("weff_lo_ready")
        weff_lo_ready_v = sem("weff_lo_ready_v")
        weff_used = sem("weff_used")
        m_acc = sem("m_acc")
        m_raw = sem("m_raw")
        row_hi = sem("row_hi")
        row_lo_v = sem("row_lo_v")
        row_lo_g = sem("row_lo_g")
        m_hi_ready = sem("m_hi_ready")
        m_lo_ready = sem("m_lo_ready")
        ut_mm = sem("ut_mm")
        ut_sb = sem("ut_sb")
        u_back = sem("u_back")
        u_hi_ready = sem("u_hi_ready")
        u_lo_ready = sem("u_lo_ready")
        x_hi_ready = sem("x_hi_ready")
        x_lo_ready = sem("x_lo_ready")
        b_hi_ready = sem("b_hi_ready")
        b_lo_ready = sem("b_lo_ready")
        u_st_ready = sem("u_st_ready")
        p_mm = sem("p_mm")
        p_hi_ready = sem("p_hi_ready")
        p_lo_ready = sem("p_lo_ready")
        y_mm = sem("y_mm")
        y_act = sem("y_act")
        y_dve = sem("y_dve")

        block = ctx.enter_context(nc.Block())

        B0, A0, A1 = [("b0", 0), ("b0", 1)], [("a0", 0), ("a0", 1)], ("a1", 0)
        W = [("w", t) for t in range(DT)]
        SLOT = {"b0": 0, "a0": 1, "a1": 2, "w": 3}
        SPLITS = [B0[0], A0[0], B0[1], W[0], A0[1], W[1], W[2], W[3], A1] + W[4:]
        BY_POOL = [B0[0], A0[0], B0[1], W[0], W[3]]
        BY_VECTOR = [A0[1], W[1], W[2], A1, W[4], W[5], W[6], W[7]]
        MASK_ORDER = [0, 4, 1, 5, 2, 6, 3]
        LAST = STEPS - 1

        LATE_ROWS = range(DT - QI)
        LATE_BY_POOL, LATE_BY_VECTOR = [2, 5], [0, 1, 3, 4]

        def upper_by_act(k):
            return 2 <= k <= 5

        def low_by_vector(k):
            return range(OP) if k == LAST else [OP - 1] if k >= NJ and k % 2 == 0 else []

        def slot(piece):
            return SLOT[piece[0]] + (piece[1] if piece[0] == "w" else 0)

        def columns(piece):
            return (slice(0, QC), slice(QC, D))[piece[1]] if piece[0] in ("a0", "b0") else slice(0, D)

        def staged(piece, rows=slice(0, P)):
            s = stage[rows, slot(piece), columns(piece)]
            return s.rearrange("p (b t r) -> p t b r", b=NB, t=DT) if piece == A1 else s

        def split_to(piece, t, rows=slice(0, P)):
            if piece == A1:
                return t[:].rearrange("p t (b r) -> p t b r", b=NB)
            return t[rows, piece[1], :] if piece[0] == "w" else t[rows, columns(piece)]

        HIGH_OF = {"b0": b0_hl, "a0": a0_hi, "a1": a1_hi, "w": w_hi}
        LOW_OF = {"b0": b0_hl, "a0": a0_lo, "a1": a1_lo, "w": w_lo}

        def stage_wait(eng, piece):
            loads = NB if piece == A1 else 1
            done = staged_in[slot(piece)] if piece[1] == 0 or piece[0] == "w" else rest_in[slot(piece)]
            eng.wait_ge(done, 16 * loads)

        def high_wait(eng, piece):
            eng.wait_ge(hi_made, SPLITS.index(piece) + 1)

        def low_wait(eng, piece):
            if piece in BY_POOL:
                eng.wait_ge(lo_made_g, BY_POOL.index(piece) + 1)
            else:
                eng.wait_ge(lo_made_v, BY_VECTOR.index(piece) + 1)

        def scales(t, k):
            q, j = k // NJ, k % NJ
            t = t[:].rearrange("p (t g) -> p t g", g=G)[:, j * OP:(j + 1) * OP, q * QI:(q + 1) * QI]
            return t.unsqueeze(3).broadcast_to([P, OP, QI, P])

        def row_tile(t):
            return slice(t * QC, (t + 1) * QC)

        def weff_wait(eng, k, t=OP - 1):
            if k == LAST:
                eng.wait_ge(weff_ready, OP * LAST)
                eng.wait_ge(weff_ready_v, t + 1)
            else:
                eng.wait_ge(weff_ready, OP * k + t + 1)

        def weff_used_wait(eng, k):
            if k % NJ == NJ - 1:
                eng.wait_ge(m_acc, 4 * (k // NJ + 1))
            else:
                eng.wait_ge(weff_used, k - k // NJ + 1)

        def weff_hi_wait(eng, k, t=OP - 1):
            eng.wait_ge(weff_hi_ready, OP * k + t + 1)

        def weff_lo_wait(eng, k):
            by_vector = sum(len(low_by_vector(n)) for n in range(k + 1))
            eng.wait_ge(weff_lo_ready, OP * (k + 1) - by_vector)
            if by_vector:
                eng.wait_ge(weff_lo_ready_v, by_vector)

        PAIRS = (NB - 2) // 2

        def first(b, n=1):
            return isinstance(b, int) and b < n

        def y_bank(b, tt, h):
            if first(b) and tt == 0:
                return ps_d[h][:].rearrange("p t c -> p (t c)")
            return acc[2 * tt + h][:]

        @block.sync
        def _(sp):
            def load_factor(name, src, n):
                done = (staged_in, rest_in)[n][SLOT[name]]
                c = columns((name, n))
                sp.dma_start(stage[:, SLOT[name], c], src[:, c]).then_inc(done, 16)

            def load_w(t):
                sp.dma_start(stage[:, slot(W[t]), :], w1[t * P:(t + 1) * P, :]).then_inc(staged_in[slot(W[t])], 16)

            def load_a1(b):
                e = sp.value_load(ids[0:1, b:b + 1], min_val=0, max_val=NA - 1)
                sp.dma_start(stage[:, slot(A1), b * DT * R1:(b + 1) * DT * R1],
                             lora1_a[bass.ds(e, 1), :, :].rearrange("a p c -> (a p) c")
                             ).then_inc(staged_in[slot(A1)], 16)

            def load_weight(k):
                q, j = k // NJ, k % NJ
                if k >= 2:
                    sp.wait_ge(wsum, k - 1)
                sp.dma_start(wraw[:, k % 2, :, :], weightT[j, :, :, q * QC:(q + 1) * QC]
                             ).then_inc(weight_in[k % 2], 16)

            sp.dma_start(ex[:, 0, :], scale_log).then_inc(scale_log_in, 16)
            sp.dma_start(cbt[:], codebook).then_inc(codebook_in, 16)
            load_factor("b0", lora0_bT, 0)
            load_factor("a0", lora0_a, 0)
            load_weight(0)
            load_factor("b0", lora0_bT, 1)
            load_w(0)
            load_weight(1)
            load_factor("a0", lora0_a, 1)
            sp.dma_start(ids[:], adapter).then_inc(ids_in, 16)
            for t in range(1, 4):
                load_w(t)
            sp.wait_ge(ids_in, 16)
            for b in range(NB):
                load_a1(b)
                if b % 2:
                    load_w(4 + b // 2)
                if b == 1:
                    load_weight(2)
            for k in range(3, STEPS):
                load_weight(k)

            def load_x(b, slot):
                sp.dma_start(x_raw[:, slot, :], xT[bass.ds(b, 1), :, :].rearrange(
                    "b p c -> (b p) c")).then_inc(x_in[slot], 16)

            def load_b(b):
                e = sp.value_load(ids[0:1, bass.ds(b, 1)], min_val=0, max_val=NA - 1)
                src = lora1_b[bass.ds(e, 1), :, :].rearrange("a r n -> (a r) n")
                for g in range(P // R1):
                    sp.dma_start(b_raw[g * R1:(g + 1) * R1, :], src).then_inc(b_in, 16)

            def store(b, tt):
                sp.wait_ge(y_act, b * TT + tt + 1)
                sp.wait_ge(y_dve, b * TT + tt + 1)
                sp.dma_start(out[bass.ds(b * TT + tt, 1), :, :].rearrange("t p n -> (t p) n"),
                             y[:, tt, :]).then_inc(y_out[tt], 16)

            def store_last_tile():
                dst = out[NB * TT - 1, :, :]
                for h, copied in enumerate((y_act, y_dve)):
                    cols = slice(h * HB, (h + 1) * HB)
                    sp.wait_ge(copied, NB * TT)
                    sp.dma_start(dst[:, cols], y[:, TT - 1, cols]).then_inc(y_out[TT - 1], 16)

            def next_b(b):
                sp.wait_ge(b_hi_ready, b + 1)
                sp.wait_ge(b_lo_ready, b + 1)
                load_b(b + 1)

            def next_x(b, slot):
                sp.wait_ge(x_hi_ready, b + 1)
                sp.wait_ge(x_lo_ready, b + 1)
                load_x(b + 2, slot)

            sp.wait_ge(delta_mm, STEPS)
            load_x(0, 0)
            weff_wait(sp, LAST)
            load_x(1, 1)
            load_b(0)
            with sp.Fori(0, PAIRS) as r:
                for u in range(2):
                    b = 2 * r + u
                    next_b(b)
                    next_x(b, u)
                    for tt in range(TT):
                        store(b, tt)
            next_b(NB - 2)
            for tt in range(TT):
                store(NB - 2, tt)
            for tt in range(TT - 1):
                store(NB - 1, tt)
            store_last_tile()
            for tt in range(TT):
                sp.wait_ge(y_out[tt], 16 * (NB + (tt == TT - 1)))

        @block.gpsimd
        def _(pool):
            g = nc.gpsimd
            chain = [0]

            def link(ins):
                chain[0] += 1
                ins.then_inc(gchain, 1)
                pool.wait_ge(gchain, chain[0])

            link(g.memset(ident[:], 0.0))
            g.affine_select(out=ident[:], in_=ident[:], compare_op=ALU.not_equal, fill=1.0, base=0,
                            pattern=[[-1, P]], channel_multiplier=1).then_inc(ident_made, 1)
            pool.wait_ge(ident_made, 1)

            def diag(t):
                stage_wait(pool, W[t])
                d = stage[:, slot(W[t]), t * P:(t + 1) * P]
                g.tensor_tensor(d, d, ident[:], ALU.add).then_inc(diag_added, 1)

            def low(piece, rows=slice(0, P)):
                high_wait(pool, piece)
                g.tensor_tensor(split_to(piece, LOW_OF[piece[0]], rows), staged(piece, rows),
                                split_to(piece, HIGH_OF[piece[0]], rows).bitcast(f32),
                                ALU.subtract).then_inc(lo_made_g, 1)

            low(B0[0], slice(R0, P))
            low_wait(pool, B0[0])
            low(A0[0])
            low_wait(pool, A0[0])
            diag(0)
            pool.wait_ge(diag_added, 1)
            low(B0[1], slice(R0, P))
            low_wait(pool, B0[1])
            low(W[0])
            for t in range(1, 4):
                diag(t)

            def low_weff(k):
                if k >= 3:
                    weff_used_wait(pool, k - 3)
                for t in [t for t in range(OP) if t not in low_by_vector(k)]:
                    weff_hi_wait(pool, k, t)
                    g.tensor_tensor(weff_lo[:, k % 3, t, :], quan[:, k % 3, row_tile(t)],
                                    weff_hi[:, k % 3, t, :].bitcast(f32), ALU.subtract).then_inc(weff_lo_ready, 1)

            def dequantise(k):
                v = quan[:, k % 3, :]
                pool.wait_ge(select_done, 8 * (k + 1))
                link(g.tensor_tensor(v, v, norm[:, k % 3, :], ALU.subtract))
                link(g.tensor_tensor(v, v, norm[:, k % 3, :], ALU.add))
                v4 = v.rearrange("p (t g c) -> p t g c", t=OP, g=QI)
                link(g.tensor_tensor(v4, v4, scales(scale, k), ALU.mult))
                pool.wait_ge(delta_sb, k + 1)
                diagonal = k // NJ == k % NJ
                for t in range(OP):
                    w = v[:, row_tile(t)]
                    ins = g.tensor_tensor(w, w, delta[:, k % 4, row_tile(t)], ALU.add)
                    if diagonal:
                        link(ins)
                        w = w[:, t * P:(t + 1) * P]
                        ins = g.tensor_tensor(w, w, ident[:], ALU.add)
                    ins.then_inc(weff_ready, 1)

            pool.wait_ge(scale_ready, 1)
            for k in range(LAST):
                if k:
                    low_weff(k - 1)
                if k == 1:
                    low(W[3])
                dequantise(k)
                if k in (0, 1):
                    diag(2 * k + 4)
                    diag(2 * k + 5)
            low_weff(LAST - 1)
            for i in LATE_BY_POOL:
                pool.wait_ge(row_hi, i + 1)
                g.tensor_tensor(m_lo[:, i, :], m_whole[:, i, :], m_hi[:, i, :].bitcast(f32),
                                ALU.subtract).then_inc(row_lo_g, 1)

        @block.scalar
        def _(act):
            a = nc.scalar

            def high(piece):
                stage_wait(act, piece)
                if piece[0] == "w":
                    act.wait_ge(diag_added, piece[1] + 1)
                a.activation(split_to(piece, HIGH_OF[piece[0]]), staged(piece), ACT.Copy).then_inc(hi_made, 1)

            def copy_delta(k):
                act.wait_ge(delta_mm, k + 1)
                if k >= 4:
                    weff_wait(act, k - 4)
                a.activation(delta[:, k % 4, :], ps_d[k % 2][:].rearrange("p t c -> p (t c)"), ACT.Copy,
                             scale=0.5).then_inc(delta_sb, 1)

            def masks(k, order):
                act.wait_ge(norm_ready, k + 1)
                if k >= 2:
                    act.wait_ge(select_done, 8 * (k - 1))
                for i in order:
                    a.activation(mask[:, k % 2, i, :], norm[:, k % 3, :], ACT.Sign,
                                 bias=negbrk[:, i:i + 1]).then_inc(mask_ready, 1)

            def start_upper(k):
                act.wait_ge(select_done, 8 * k)
                a.activation(upper[:], cbn[:, 4:5].broadcast_to([P, SE]), ACT.Copy).then_inc(upper_started, 1)

            def high_weff(k):
                if k >= 3:
                    weff_used_wait(act, k - 3)
                    weff_lo_wait(act, k - 3)
                for t in range(OP):
                    weff_wait(act, k, t)
                    a.activation(weff_hi[:, k % 3, t, :], quan[:, k % 3, row_tile(t)],
                                 ACT.Copy).then_inc(weff_hi_ready, 1)

            def bank_of_m(t, q, bank):
                return t[:, q * QI + bank // 2, bank % 2 * HB:(bank % 2 + 1) * HB]

            def take_m(q, bank):
                act.wait_ge(m_acc, 4 * q + bank + 1)
                a.activation(bank_of_m(m_whole, q, bank), acc[bank][:], ACT.Copy).then_inc(m_raw, 1)

            def high_row(i):
                act.wait_ge(m_raw, 2 * (i + 1))
                a.activation(m_hi[:, i, :], m_whole[:, i, :], ACT.Copy).then_inc(row_hi, 1)

            def high_m(bank):
                act.wait_ge(m_acc, 4 * (NQ - 1) + bank + 1)
                a.activation(bank_of_m(m_hi, NQ - 1, bank), acc[bank][:], ACT.Copy).then_inc(m_hi_ready, 1)

            def take_ut(q):
                act.wait_ge(ut_mm, q + 1)
                if q:
                    act.wait_ge(u_back, q)
                a.activation(ut[:], ps_u[:, 0:QC], ACT.Copy).then_inc(ut_sb, 1)

            def high_u(q):
                act.wait_ge(u_back, q + 1)
                a.activation(u_hi[:, q * QI:(q + 1) * QI, :],
                             ps_t[:, 0:QC].rearrange("p (t c) -> p t c", t=QI), ACT.Copy).then_inc(u_hi_ready, 1)

            high(B0[0])
            high(A0[0])
            high(B0[1])
            copy_delta(0)
            high(W[0])
            act.wait_ge(brk_ready, 1)
            for k in range(STEPS + 1):
                if k and k + 2 < STEPS:
                    copy_delta(k + 2)
                ending = k - NJ - 1 if k > NJ and (k - NJ - 1) % NJ == 0 and k < STEPS else None
                ended = k - NJ - 2 if k > NJ + 1 and (k - NJ - 2) % NJ == 0 and k < STEPS else None
                if k < STEPS:
                    masks(k, MASK_ORDER[:1])
                    if upper_by_act(k):
                        start_upper(k)
                    if ended is not None:
                        take_m(ended // NJ, 2)
                        take_m(ended // NJ, 3)
                    masks(k, MASK_ORDER[1:4])
                    if k == 0:
                        copy_delta(1)
                    masks(k, MASK_ORDER[4:5])
                    if ended is not None:
                        take_ut(ended // NJ)
                    masks(k, MASK_ORDER[5:])
                if ending is not None:
                    take_m(ending // NJ, 0)
                if k >= LAST:
                    high_row(2 * (k - LAST))
                    high_row(2 * (k - LAST) + 1)
                if k == 0:
                    copy_delta(2)
                    high(A0[1])
                    high(W[1])
                else:
                    high_weff(k - 1)
                if ending is not None:
                    take_m(ending // NJ, 1)
                if k >= NJ and k % NJ == 0 and k // NJ >= 2:
                    high_u(k // NJ - 2)
                if 1 <= k < NJ:
                    high(W[2 * k])
                    high(W[2 * k + 1])
                if k == 1:
                    high(A1)

            def high_x(b, slot, half):
                act.wait_ge(x_in[slot], 16 * (half + 1))
                if first(b, 2):
                    if slot:
                        weff_lo_wait(act, LAST)
                else:
                    act.wait_ge(y_mm, 2 * TT * (b - 1))
                a.activation(x_hi[:, slot, :, :].rearrange("p t c -> p (t c)"), x_raw[:, slot, :],
                             ACT.Copy).then_inc(x_hi_ready, 1)

            def high_b(b, slot):
                act.wait_ge(b_in, 16 * (P // R1) * (b + 1))
                a.activation(b_hl[:, slot, :], b_raw[:], ACT.Copy).then_inc(b_hi_ready, 1)

            def stack_u(b, slot):
                if not first(b, 2):
                    act.wait_ge(p_mm, b - 1)
                for c, u in enumerate((u_hi, u_lo)):
                    src = u[:, :, bass.ds(b * R1, R1)].bitcast(f32).unsqueeze(2).broadcast_to([P, DT, 4, R1])
                    a.activation(u_st[:, slot, :, :, c, :], src, ACT.Copy).then_inc(u_st_ready, 1)

            def high_p(b, slot):
                act.wait_ge(p_mm, b + 1)
                a.activation(p_hl[:, slot, :], ps_u[:, 0:TOK], ACT.Copy).then_inc(p_hi_ready, 1)

            def copy_y(b, tt):
                act.wait_ge(y_mm, 2 * (b * TT + tt) + 1)
                if not first(b):
                    act.wait_ge(y_out[tt], 16 * b)
                a.activation(y[:, tt, 0:HB], y_bank(b, tt, 0), ACT.Copy).then_inc(y_act, 1)

            def batch(b, slot, half):
                if half is not None:
                    high_x(b + 1, 1 - slot, half)
                    stack_u(b + 1, 1 - slot)
                high_p(b, slot)
                if half is not None:
                    high_b(b + 1, 1 - slot)
                for tt in range(TT):
                    copy_y(b, tt)

            high_row(4)
            high_row(5)
            high_x(0, 0, 0)
            take_ut(NQ - 1)
            for bank in range(4):
                high_m(bank)
            high_u(NQ - 1)
            act.wait_ge(u_hi_ready, NQ)
            act.wait_ge(u_lo_ready, NQ)
            stack_u(0, 0)
            high_b(0, 0)
            batch(0, 0, 0)
            with act.Fori(0, PAIRS) as r:
                batch(2 * r + 1, 1, r + 1)
                batch(2 * r + 2, 0, r + 1)
            batch(NB - 1, 1, None)

        @block.vector
        def _(dve):
            v = nc.vector
            chain = [0]

            def low(piece):
                high_wait(dve, piece)
                v.tensor_tensor(split_to(piece, LOW_OF[piece[0]]), staged(piece),
                                split_to(piece, HIGH_OF[piece[0]]).bitcast(f32),
                                ALU.subtract).then_inc(lo_made_v, 1)

            def turn(ins):
                chain[0] += 1
                ins.then_inc(vchain, 1)
                if chain[0] > 1:
                    dve.wait_ge(vchain, chain[0] - 1)

            x_, r_, p_ = ex[:, 0, :], ex[:, 1, :], ex[:, 2, :]

            def horner(c):
                return v.scalar_tensor_tensor(out=p_, in0=p_, scalar=c, in1=r_, op0=ALU.add, op1=ALU.mult)

            dve.wait_ge(scale_log_in, 16)
            dve.wait_ge(codebook_in, 16)
            turn(v.tensor_scalar(x_, x_, -104.0, 89.5, ALU.max, ALU.min))
            turn(v.tensor_scalar(cbn[:], cbt[:], -1.0, None, ALU.mult))
            turn(v.tensor_scalar(ki[:, 1, :], x_, 1.4426950408889634, None, ALU.mult))
            turn(v.tensor_tensor(cbn[:], cbn[:], cbt[:], ALU.max))
            turn(v.tensor_copy(p_, ki[:, 1, :]))
            turn(v.reduce_max(cbmax[:, 0:1], cbn[:], AX.X))
            turn(v.scalar_tensor_tensor(out=r_, in0=p_, scalar=-0.693359375, in1=x_, op0=ALU.mult, op1=ALU.add))
            turn(v.tensor_scalar(cbmax[:, 0:1], cbmax[:, 0:1], 1e-8, None, ALU.max))
            turn(v.scalar_tensor_tensor(out=r_, in0=p_, scalar=2.12194440e-4, in1=r_, op0=ALU.mult, op1=ALU.add))
            turn(v.reciprocal(cbmax[:, 1:2], cbmax[:, 0:1]))
            turn(v.tensor_scalar(p_, r_, 1.0 / 5040, None, ALU.mult))
            turn(v.tensor_scalar(cbn[:], cbt[:], cbmax[:, 1:2], None, ALU.mult))
            turn(horner(1.0 / 720))
            turn(v.tensor_tensor(thr[:], cbn[:, 0:NL - 1], cbn[:, 1:NL], ALU.add))
            turn(horner(1.0 / 120))
            turn(v.tensor_scalar(thr[:], thr[:], 0.5, None, ALU.mult))
            turn(horner(1.0 / 24))
            turn(v.tensor_copy(brk[:, 3:4], thr[:, 3:4]))
            turn(horner(1.0 / 6))
            turn(v.tensor_tensor(brk[:, 1:2], thr[:, 1:2], brk[:, 3:4], ALU.min))
            turn(horner(0.5))
            turn(v.tensor_tensor(brk[:, 5:6], thr[:, 5:6], brk[:, 3:4], ALU.max))
            turn(horner(1.0))
            turn(v.tensor_scalar(ki[:, 0, :], ki[:, 1, :], 1, None, ALU.arith_shift_right))
            turn(v.tensor_scalar(p_, p_, 1.0, None, ALU.add))
            turn(v.tensor_tensor(ki[:, 1, :], ki[:, 1, :], ki[:, 0, :], ALU.subtract))
            turn(v.tensor_tensor(brk[:, 2:5:2], thr[:, 2:5:2], brk[:, 1:4:2], ALU.max))
            turn(v.tensor_scalar(kb[:], ki[:], 127.0, None, ALU.add))
            turn(v.tensor_tensor(brk[:, 2:5:2], brk[:, 2:5:2], brk[:, 3:6:2], ALU.min))
            turn(v.tensor_scalar(kb[:], kb[:], 23, None, ALU.logical_shift_left))
            turn(v.tensor_tensor(brk[:, 0:1], thr[:, 0:1], brk[:, 1:2], ALU.min))
            turn(v.tensor_tensor(p_, p_, kb[:, 0, :].bitcast(f32), ALU.mult))
            turn(v.tensor_tensor(brk[:, 6:7], thr[:, 6:7], brk[:, 5:6], ALU.max))
            turn(v.tensor_tensor(scale[:], p_, kb[:, 1, :].bitcast(f32), ALU.mult))
            v.tensor_scalar(negbrk[:], brk[:], -1.0, None, ALU.mult).then_inc(brk_ready, 1)
            dve.wait_ge(vchain, chain[0])
            v.reciprocal(rscale[:], scale[:]).then_inc(scale_ready, 1)
            dve.wait_ge(scale_ready, 1)

            def add_weight(k):
                dve.wait_ge(delta_sb, k + 1)
                dve.wait_ge(weight_in[k % 2], 16 * (k // 2 + 1))
                if k >= 3:
                    weff_wait(dve, k - 3)
                v.tensor_tensor(norm[:, k % 3, :], delta[:, k % 4, :],
                                wraw[:, k % 2, :, :].rearrange("p t c -> p (t c)"), ALU.add).then_inc(wsum, 1)

            def over_scale(k):
                dve.wait_ge(wsum, k + 1)
                n4 = norm[:, k % 3, :].rearrange("p (t g c) -> p t g c", t=OP, g=QI)
                v.tensor_tensor(n4, n4, scales(rscale, k), ALU.mult).then_inc(norm_ready, 1)

            def start(k):
                if k >= 3:
                    weff_lo_wait(dve, k - 3)
                    weff_hi_wait(dve, k - 3)
                v.tensor_copy(quan[:, k % 3, :], cbn[:, 0:1].broadcast_to([P, SE])).then_inc(select_done, 1)
                if not upper_by_act(k):
                    if k:
                        dve.wait_ge(select_done, 8 * k)
                    v.tensor_copy(upper[:], cbn[:, 4:5].broadcast_to([P, SE])).then_inc(upper_started, 1)

            def select(k):
                lower = quan[:, k % 3, :]
                for n, i in enumerate(MASK_ORDER):
                    dve.wait_ge(mask_ready, 7 * k + n + 1)
                    if n == 1:
                        dve.wait_ge(upper_started, k + 1)
                    else:
                        dve.wait_ge(select_done, 8 * k + max(n, 1) + (i == 3))
                    dst = upper[:] if i > 3 else lower
                    data = upper[:] if i == 3 else cbn[:, i + 1:i + 2].broadcast_to([P, SE])
                    v.copy_predicated(dst, mask[:, k % 2, i, :], data).then_inc(select_done, 1)

            def low_weff(k):
                for t in low_by_vector(k):
                    weff_hi_wait(dve, k, t)
                    weff_used_wait(dve, k - 3)
                    v.tensor_tensor(weff_lo[:, k % 3, t, :], quan[:, k % 3, row_tile(t)],
                                    weff_hi[:, k % 3, t, :].bitcast(f32), ALU.subtract).then_inc(weff_lo_ready_v, 1)

            def dequantise_last():
                k = LAST
                t = quan[:, k % 3, :]
                t4 = t.rearrange("p (t g c) -> p t g c", t=OP, g=QI)
                dve.wait_ge(select_done, 8 * (k + 1))
                v.tensor_tensor(t, t, norm[:, k % 3, :], ALU.subtract).then_inc(last_chain, 1)
                dve.wait_ge(last_chain, 1)
                v.tensor_tensor(t, t, norm[:, k % 3, :], ALU.add).then_inc(last_chain, 1)
                dve.wait_ge(last_chain, 2)
                v.tensor_tensor(t4, t4, scales(scale, k), ALU.mult).then_inc(last_chain, 1)
                dve.wait_ge(last_chain, 3)
                for i in range(OP):
                    w = t[:, row_tile(i)]
                    v.tensor_tensor(w, w, delta[:, k % 4, row_tile(i)], ALU.add).then_inc(last_chain, 1)
                dve.wait_ge(ident_made, 1)
                for i in range(OP):
                    dve.wait_ge(last_chain, 4 + i)
                    w = t[:, i * QC + i * P:i * QC + (i + 1) * P]
                    v.tensor_tensor(w, w, ident[:], ALU.add).then_inc(weff_ready_v, 1)

            def low_row(i):
                dve.wait_ge(row_hi, i + 1)
                v.tensor_tensor(m_lo[:, i, :], m_whole[:, i, :], m_hi[:, i, :].bitcast(f32),
                                ALU.subtract).then_inc(row_lo_v, 1)

            def low_m(bank):
                dve.wait_ge(m_hi_ready, bank + 1)
                i, h = (NQ - 1) * QI + bank // 2, slice(bank % 2 * HB, (bank % 2 + 1) * HB)
                v.tensor_tensor(m_lo[:, i, h], acc[bank][:], m_hi[:, i, h].bitcast(f32),
                                ALU.subtract).then_inc(m_lo_ready, 1)

            def low_u(q):
                dve.wait_ge(u_hi_ready, q + 1)
                v.tensor_tensor(u_lo[:, q * QI:(q + 1) * QI, :],
                                ps_t[:, 0:QC].rearrange("p (t c) -> p t c", t=QI),
                                u_hi[:, q * QI:(q + 1) * QI, :].bitcast(f32), ALU.subtract).then_inc(u_lo_ready, 1)

            add_weight(0)
            over_scale(0)
            start(0)
            select(0)
            add_weight(1)
            over_scale(1)
            low(A0[1])
            low(W[1])
            for k in range(1, STEPS):
                if k + 1 < STEPS:
                    add_weight(k + 1)
                if k >= 2:
                    low_weff(k - 2)
                start(k)
                if k + 1 < STEPS:
                    over_scale(k + 1)
                if k == 2:
                    low(A1)
                if k > 2 * NJ and (k - 1) % NJ == 0:
                    low_u((k - 1) // NJ - 2)
                select(k)
                if k < NJ:
                    low(W[2 * k])
                    if k > 1:
                        low(W[2 * k + 1])
            low_weff(LAST - 1)
            dequantise_last()
            low_weff(LAST)

            def low_x(b, slot):
                dve.wait_ge(x_hi_ready, b + 1)
                v.tensor_tensor(x_lo[:, slot, :, :].rearrange("p t c -> p (t c)"), x_raw[:, slot, :],
                                x_hi[:, slot, :, :].rearrange("p t c -> p (t c)").bitcast(f32),
                                ALU.subtract).then_inc(x_lo_ready, 1)

            def low_b(b, slot):
                dve.wait_ge(b_hi_ready, b + 1)
                v.tensor_tensor(b_hl[P // 2:P, slot, :], b_raw[P // 2:P, :],
                                b_hl[P // 2:P, slot, :].bitcast(f32), ALU.subtract).then_inc(b_lo_ready, 1)

            def low_p(b, slot):
                dve.wait_ge(p_hi_ready, b + 1)
                for g in (1, 3):
                    s = slice(32 * g, 32 * g + 32)
                    v.tensor_tensor(p_hl[s, slot, :], ps_u[s, 0:TOK], p_hl[s, slot, :].bitcast(f32),
                                    ALU.subtract).then_inc(p_lo_ready, 1)

            def copy_y(b, tt):
                dve.wait_ge(y_mm, 2 * (b * TT + tt) + 2)
                if not first(b):
                    dve.wait_ge(y_out[tt], 16 * b)
                v.tensor_copy(y[:, tt, HB:D], y_bank(b, tt, 1)).then_inc(y_dve, 1)

            def batch(b, slot, more=True):
                if more:
                    low_x(b + 1, 1 - slot)
                low_p(b, slot)
                if more:
                    low_b(b + 1, 1 - slot)
                for tt in range(TT):
                    copy_y(b, tt)

            low_u(NQ - 2)
            for i in LATE_BY_VECTOR:
                low_row(i)
            low_x(0, 0)
            for bank in range(4):
                low_m(bank)
            low_u(NQ - 1)
            low_b(0, 0)
            batch(0, 0)
            with dve.Fori(0, PAIRS) as r:
                batch(2 * r + 1, 1)
                batch(2 * r + 2, 0)
            batch(NB - 1, 1, more=False)

        @block.tensor
        def _(pe):
            t_ = nc.tensor

            def delta_product(k):
                q, j = k // NJ, k % NJ
                if k >= 2:
                    pe.wait_ge(delta_sb, k - 1)
                for t in range(OP):
                    rows = b0_hl[:, (j * OP + t) * P:(j * OP + t + 1) * P]
                    for n, a0 in enumerate((a0_hi, a0_lo)):
                        last = t_.matmul(ps_d[k % 2][:, t, :], rows, a0[:, q * QC:(q + 1) * QC],
                                         start=(n == 0), stop=(n == 1))
                last.then_inc(delta_mm, 1)

            def w_ready(t):
                high_wait(pe, W[t])
                low_wait(pe, W[t])

            def accumulate_u(k):
                q, j = k // NJ, k % NJ
                first, last_step = j == 0, j == NJ - 1
                if k == 0:
                    low_wait(pe, A1)
                if first and q:
                    pe.wait_ge(ut_sb, q)
                for t in range(OP):
                    o = j * OP + t
                    hi, lo = weff_hi[:, k % 3, t, :], weff_lo[:, k % 3, t, :]
                    t_.matmul(ps_u[:, 0:QC], a1_hi[:, o, :], hi, start=first and t == 0, stop=False)
                    t_.matmul(ps_u[:, 0:QC], a1_lo[:, o, :], hi, start=False, stop=False)
                    last = t_.matmul(ps_u[:, 0:QC], a1_hi[:, o, :], lo, start=False,
                                     stop=last_step and t == OP - 1)
                last.then_inc(ut_mm if last_step else weff_used, 1)

            def accumulate(k):
                q, j = k // NJ, k % NJ
                first, last_step = j == 0, j == NJ - 1
                weff_hi_wait(pe, k)
                weff_lo_wait(pe, k)
                if q == 0:
                    for t in range(OP):
                        w_ready(j * OP + t)
                if last_step:
                    accumulate_u(k)
                for i in range(QI):
                    for h in range(2):
                        if first and q:
                            pe.wait_ge(m_raw, 4 * (q - 1) + 2 * i + h + 1)
                        bank, cols = acc[2 * i + h][:], slice(h * HB, (h + 1) * HB)
                        for t in range(OP):
                            o = j * OP + t
                            hi = weff_hi[:, k % 3, t, i * P:(i + 1) * P]
                            lo = weff_lo[:, k % 3, t, i * P:(i + 1) * P]
                            t_.matmul(bank, hi, w_hi[:, o, cols], start=first and t == 0, stop=False)
                            t_.matmul(bank, hi, w_lo[:, o, cols], start=False, stop=False)
                            last = t_.matmul(bank, lo, w_hi[:, o, cols], start=False,
                                             stop=last_step and t == OP - 1)
                        if last_step:
                            last.then_inc(m_acc, 1)
                if not last_step:
                    accumulate_u(k)

            def turn_u(q):
                pe.wait_ge(ut_sb, q + 1)
                if q:
                    pe.wait_ge(u_lo_ready, q)
                for i in range(QI):
                    last = t_.transpose(ps_t[:, i * P:(i + 1) * P], ut[:, i * P:(i + 1) * P], ident[:])
                last.then_inc(u_back, 1)

            high_wait(pe, A0[0])
            low_wait(pe, A0[0])
            low_wait(pe, B0[0])
            delta_product(0)
            high_wait(pe, B0[1])
            low_wait(pe, B0[1])
            for k in range(1, 4):
                delta_product(k)
            high_wait(pe, A0[1])
            low_wait(pe, A0[1])
            delta_product(4)
            pe.wait_ge(ident_made, 1)
            for k in range(STEPS):
                if k + 5 < STEPS:
                    delta_product(k + 5)
                accumulate(k)
                if k >= NJ and k % NJ == 0:
                    turn_u(k // NJ - 1)
            turn_u(NQ - 1)

            def tokens_times_u(b, s):
                pe.wait_ge(u_st_ready, 2 * (b + 1))
                if not first(b):
                    pe.wait_ge(p_lo_ready, 2 * b)
                    pe.wait_ge(p_hi_ready, b)
                for i in range(DT):
                    ust = u_st[:, s, i, :, :, :].rearrange("p a c r -> p (a c r)")
                    for n, xx in enumerate((x_hi, x_lo)):
                        last = t_.matmul(ps_u[:, 0:TOK], ust, xx[:, s, i, :], start=(i == 0 and n == 0),
                                         stop=(i == DT - 1 and n == 1))
                last.then_inc(p_mm, 1)

            def tokens_times_m(b, s, tt, h, tiles):
                tok, cols = slice(tt * P, (tt + 1) * P), slice(h * HB, (h + 1) * HB)
                bank = y_bank(b, tt, h)
                for i in tiles:
                    t_.matmul(bank, x_hi[:, s, i, tok], m_hi[:, i, cols], start=(i == 0), stop=False)
                    t_.matmul(bank, x_hi[:, s, i, tok], m_lo[:, i, cols], start=False, stop=False)
                    t_.matmul(bank, x_lo[:, s, i, tok], m_hi[:, i, cols], start=False, stop=False)

            def add_lora(b, s, tt, h):
                tok, cols = slice(tt * P, (tt + 1) * P), slice(h * HB, (h + 1) * HB)
                pe.wait_ge(p_lo_ready, 2 * (b + 1))
                pe.wait_ge(b_lo_ready, b + 1)
                t_.matmul(y_bank(b, tt, h), p_hl[:, s, tok], b_hl[:, s, cols], start=False,
                          stop=True).then_inc(y_mm, 1)

            pe.wait_ge(x_hi_ready, 1)
            pe.wait_ge(x_lo_ready, 1)
            pe.wait_ge(delta_sb, STEPS)
            for i in LATE_ROWS:
                if i in LATE_BY_POOL:
                    pe.wait_ge(row_lo_g, LATE_BY_POOL.index(i) + 1)
                else:
                    pe.wait_ge(row_lo_v, LATE_BY_VECTOR.index(i) + 1)
                tokens_times_m(0, 0, 0, 0, [i])
            tokens_times_m(0, 0, 0, 1, LATE_ROWS)
            pe.wait_ge(m_hi_ready, 4)
            pe.wait_ge(m_lo_ready, 4)
            for h in range(2):
                tokens_times_m(0, 0, 0, h, range(DT - QI, DT))
            tokens_times_m(0, 0, 1, 0, range(DT))
            tokens_times_u(0, 0)
            tokens_times_m(0, 0, 1, 1, range(DT))
            for tt in range(TT):
                for h in range(2):
                    add_lora(0, 0, tt, h)

            def batch(b, slot):
                pe.wait_ge(x_hi_ready, b + 1)
                pe.wait_ge(x_lo_ready, b + 1)
                tokens_times_u(b, slot)
                for tt in range(TT):
                    for h in range(2):
                        pe.wait_ge(y_dve if h else y_act, TT * (b - 1) + tt + 1)
                        tokens_times_m(b, slot, tt, h, range(DT))
                        add_lora(b, slot, tt, h)

            with pe.Fori(0, PAIRS) as r:
                batch(2 * r + 1, 1)
                batch(2 * r + 2, 0)
            batch(NB - 1, 1)


def kernel(x, condB_codebook, itok_B_0_15, L0_cond_weight, L0_cond_scale_log, L0_cond_lora_A,
           L0_cond_lora_B, L1_cond_W, L1_cond_lora_A, L1_cond_lora_B):
    import numpy as np
    import concourse.bacc as bacc
    from concourse import mybir
    from concourse.bass_utils import run_bass_kernel_spmd

    B, S, D = x.shape
    T = D // P
    NA, _, R = L1_cond_lora_A.shape
    laid = {
        "xT": np.asarray(x).reshape(B, S, T, P).transpose(0, 3, 2, 1).reshape(B, P, T * S),
        "codebook": np.tile(np.asarray(condB_codebook)[None, :], (P, 1)),
        "adapter": np.asarray(itok_B_0_15).reshape(1, B),
        "weight": np.asarray(L0_cond_weight).reshape(T // 2, 2, P, D).transpose(0, 2, 1, 3),
        "scale_log": np.asarray(L0_cond_scale_log).reshape(T, P, -1).transpose(1, 0, 2).reshape(P, -1),
        "lora0_a": np.tile(np.asarray(L0_cond_lora_A), (2, 1)),
        "lora0_bT": np.tile(np.asarray(L0_cond_lora_B).T, (2, 1)),
        "w1": np.asarray(L1_cond_W),
        "lora1_a": np.asarray(L1_cond_lora_A).reshape(NA, T, P, R).transpose(0, 2, 1, 3).reshape(NA, P, T * R),
        "lora1_b": np.asarray(L1_cond_lora_B),
    }
    nc = bacc.Bacc("TRN2", target_bir_lowering=False, num_devices=1)
    arrays, args = {}, []
    for name, a in laid.items():
        a = np.ascontiguousarray(a)
        arrays[name] = a
        args.append(nc.dram_tensor(name, a.shape, mybir.dt.from_np(a.dtype), kind="ExternalInput").ap())
    args.append(nc.dram_tensor("y_out", (B * S // P, P, D), mybir.dt.float32, kind="ExternalOutput").ap())
    two_layers(nc, *args)
    r = run_bass_kernel_spmd(nc, [arrays], core_ids=[0])
    return r.results[0]["y_out"].reshape(B, S, D)
```
